# Optimizing a Trainium2 kernel written in Bass

```python
import numpy as np
import jax
import jax.numpy as jnp

def _softmax(x, axis=-1):
    return jax.nn.softmax(x, axis=axis)

def _gelu(x):
    return jax.nn.gelu(x, approximate=True)

def _silu(x):
    return jax.nn.silu(x)

def _sigmoid(x):
    return jax.nn.sigmoid(x)

def _layernorm(x, axis=-1, eps=1e-05):
    m = jnp.mean(x, axis=axis, keepdims=True)
    v = jnp.var(x, axis=axis, keepdims=True)
    return (x - m) / jnp.sqrt(v + eps)

def _scatter_add(tgt, idx, src, axis=0):
    return tgt.at[idx].add(src)

def _segment_sum(src, seg, n):
    return jax.ops.segment_sum(src, seg, n)
kernel_name = 'mk_xattn_ffn_d1_seqx_r8_3265c2'

def setup_inputs(seed: int=0):
    np.random.seed(seed)
    _w = jnp.asarray

    def _rec_inputs():
        import jax
        import jax.numpy as jnp
        _rk = jax.random.key(seed)
        x = 7.22e-05 + 1 * jax.random.normal(jax.random.fold_in(_rk, 1), (32, 128, 128), jnp.float32)
        _lenS = 128 - jax.random.randint(jax.random.fold_in(_rk, 7), (32,), 0, max(1, 128 // 4) + 1, jnp.int32)
        _lenS2 = 128 - jax.random.randint(jax.random.fold_in(_rk, 8), (32,), 0, max(1, 128 // 4) + 1, jnp.int32)
        _ctx_1024P = jax.random.normal(jax.random.fold_in(_rk, 11), (32, 16, 128), jnp.float32)
        _ctx_1024c = jax.random.dirichlet(jax.random.fold_in(_rk, 511), 0.3 * jnp.ones((16,), jnp.float32), (32, 128))
        _ctx_1024t = jnp.einsum('bsk,bkd->bsd', _ctx_1024c, _ctx_1024P)
        _ctx_1024t = _ctx_1024t * jax.lax.rsqrt(jnp.mean(jnp.square(_ctx_1024t)) + 1e-12) * 0.953939
        ctx_1024 = 4.13588e-05 + 0.999923 * (_ctx_1024t + 0.3 * jax.random.normal(jax.random.fold_in(_rk, 611), (32, 128, 128), jnp.float32))
        return (x, ctx_1024)
    x, ctx_1024 = _rec_inputs()

    def _L0_xattn_setup():
        import jax, jax.numpy as jnp
        import numpy as np
        D_MODEL = 128
        H = 16
        D_K = D_MODEL // H
        B = 4
        S = 256
        key = jax.random.key(seed)
        ks = jax.random.split(key, 11)
        s = 1.0 / np.sqrt(D_MODEL)
        return {'q': jax.random.normal(ks[0], (B, S, D_MODEL), jnp.float32), 'k': jax.random.normal(ks[1], (B, S, D_MODEL), jnp.float32), 'v': jax.random.normal(ks[2], (B, S, D_MODEL), jnp.float32), 'w_q': jax.random.normal(ks[3], (D_MODEL, D_MODEL), jnp.float32) * s, 'b_q': jnp.zeros((D_MODEL,), jnp.float32), 'w_k': jax.random.normal(ks[4], (D_MODEL, D_MODEL), jnp.float32) * s, 'b_k': jnp.zeros((D_MODEL,), jnp.float32), 'w_v': jax.random.normal(ks[5], (D_MODEL, D_MODEL), jnp.float32) * s, 'b_v': jnp.zeros((D_MODEL,), jnp.float32), 'w_o': jax.random.normal(ks[6], (D_MODEL, D_MODEL), jnp.float32) * s, 'b_o': jnp.zeros((D_MODEL,), jnp.float32)}
    _L0_xattn_all = _L0_xattn_setup()
    _L0_xattn_in = {k: v for k, v in _L0_xattn_all.items() if k in ('w_q', 'b_q', 'w_k', 'b_k', 'w_v', 'b_v', 'w_o', 'b_o')}
    del _L0_xattn_all

    def _L0_ffn_setup():
        import jax, jax.numpy as jnp
        import numpy as np
        B, S, H = (2, 256, 128)
        E, I, K = (8, 512, 2)

        def _moe_forward(x, gate_w, wg, wu, wd):
            b, s, h = x.shape
            x_flat = x.reshape(-1, h)
            logits = x_flat @ gate_w.T
            top_v, top_i = jax.lax.top_k(logits, K)
            probs = jax.nn.softmax(top_v.astype(jnp.float32), axis=-1).astype(logits.dtype)
            one_hot = jax.nn.one_hot(top_i, E, dtype=probs.dtype)
            combine = jnp.einsum('tk,tke->et', probs, one_hot)

            def body(acc, ws):
                wge, wue, wde, we = ws
                hidden = jax.nn.silu(x_flat @ wge.T) * (x_flat @ wue.T)
                return (acc + we[:, None] * (hidden @ wde.T), None)
            out, _ = jax.lax.scan(body, jnp.zeros_like(x_flat), (wg, wu, wd, combine))
            return out.reshape(b, s, h)
        key = jax.random.key(seed)
        ks = jax.random.split(key, 5)
        scale_h = 1.0 / np.sqrt(H)
        scale_i = 1.0 / np.sqrt(I)
        x = jax.random.normal(ks[0], (B, S, H), dtype=jnp.float32)
        gate_w = jax.random.normal(ks[1], (E, H), dtype=jnp.float32) * scale_h
        wg = jax.random.normal(ks[2], (E, I, H), dtype=jnp.float32) * scale_h
        wu = jax.random.normal(ks[3], (E, I, H), dtype=jnp.float32) * scale_h
        wd = jax.random.normal(ks[4], (E, H, I), dtype=jnp.float32) * scale_i
        return {'x': x, 'gate_w': gate_w, 'wg': wg, 'wu': wu, 'wd': wd}
    _L0_ffn_all = _L0_ffn_setup()
    _L0_ffn_in = {k: v for k, v in _L0_ffn_all.items() if k in ('gate_w', 'wg', 'wu', 'wd')}
    del _L0_ffn_all
    return {'x': x, 'ctx_1024': ctx_1024, 'L0_xattn_w_q': _L0_xattn_in['w_q'], 'L0_xattn_b_q': _L0_xattn_in['b_q'], 'L0_xattn_w_k': _L0_xattn_in['w_k'], 'L0_xattn_b_k': _L0_xattn_in['b_k'], 'L0_xattn_w_v': _L0_xattn_in['w_v'], 'L0_xattn_b_v': _L0_xattn_in['b_v'], 'L0_xattn_w_o': _L0_xattn_in['w_o'], 'L0_xattn_b_o': _L0_xattn_in['b_o'], 'L0_ffn_gate_w': _L0_ffn_in['gate_w'], 'L0_ffn_wg': _L0_ffn_in['wg'], 'L0_ffn_wu': _L0_ffn_in['wu'], 'L0_ffn_wd': _L0_ffn_in['wd']}

def reference(x, ctx_1024, L0_xattn_w_q, L0_xattn_b_q, L0_xattn_w_k, L0_xattn_b_k, L0_xattn_w_v, L0_xattn_b_v, L0_xattn_w_o, L0_xattn_b_o, L0_ffn_gate_w, L0_ffn_wg, L0_ffn_wu, L0_ffn_wd):
    import jax
    import jax.numpy as jnp

    def _L0_xattn_ref(q, k, v, w_q, b_q, w_k, b_k, w_v, b_v, w_o, b_o):
        import jax, jax.numpy as jnp
        import numpy as np
        D_MODEL = 128
        H = 16
        D_K = D_MODEL // H
        B = 4
        S = 256
        Bq, Sq, _ = q.shape
        query = q @ w_q.T + b_q
        key_ = k @ w_k.T + b_k
        value = v @ w_v.T + b_v
        query = query.reshape(Bq, Sq, H, D_K).transpose(0, 2, 1, 3)
        key_ = key_.reshape(Bq, Sq, H, D_K).transpose(0, 2, 1, 3)
        value = value.reshape(Bq, Sq, H, D_K).transpose(0, 2, 1, 3)
        scale = 1.0 / jnp.sqrt(jnp.asarray(D_K, query.dtype))
        scores = jnp.einsum('bhqd,bhkd->bhqk', query, key_) * scale
        causal = jnp.tril(jnp.ones((Sq, Sq), bool))
        scores = jnp.where(causal[None, None], scores, -jnp.inf)
        attn = jax.nn.softmax(scores, axis=-1)
        x = jnp.einsum('bhqk,bhkd->bhqd', attn, value)
        x = x.transpose(0, 2, 1, 3).reshape(Bq, Sq, H * D_K)
        return x @ w_o.T + b_o

    def _L0_ffn_ref(x, gate_w, wg, wu, wd):
        import jax, jax.numpy as jnp
        import numpy as np
        B, S, H = (2, 256, 128)
        E, I, K = (8, 512, 2)

        def _moe_forward(x, gate_w, wg, wu, wd):
            b, s, h = x.shape
            x_flat = x.reshape(-1, h)
            logits = x_flat @ gate_w.T
            top_v, top_i = jax.lax.top_k(logits, K)
            probs = jax.nn.softmax(top_v.astype(jnp.float32), axis=-1).astype(logits.dtype)
            one_hot = jax.nn.one_hot(top_i, E, dtype=probs.dtype)
            combine = jnp.einsum('tk,tke->et', probs, one_hot)

            def body(acc, ws):
                wge, wue, wde, we = ws
                hidden = jax.nn.silu(x_flat @ wge.T) * (x_flat @ wue.T)
                return (acc + we[:, None] * (hidden @ wde.T), None)
            out, _ = jax.lax.scan(body, jnp.zeros_like(x_flat), (wg, wu, wd, combine))
            return out.reshape(b, s, h)
        return _moe_forward(x, gate_w, wg, wu, wd)
    x = x + _L0_xattn_ref(_layernorm(x, axis=-1), ctx_1024, ctx_1024, L0_xattn_w_q, L0_xattn_b_q, L0_xattn_w_k, L0_xattn_b_k, L0_xattn_w_v, L0_xattn_b_v, L0_xattn_w_o, L0_xattn_b_o)
    x = x + _L0_ffn_ref(_layernorm(x, axis=-1), L0_ffn_gate_w, L0_ffn_wg, L0_ffn_wu, L0_ffn_wd)
    return x

_drawn_inputs = setup_inputs


def setup_inputs(seed=0):
    import zlib

    import numpy as np

    out = dict(_drawn_inputs(seed))
    spreads = {'L0_xattn_b_q': (0.0, 0.1),
     'L0_xattn_b_k': (0.0, 0.1),
     'L0_xattn_b_v': (0.0, 0.1),
     'L0_xattn_b_o': (0.0, 0.1)}
    factors = {}
    for name, (base, spread) in spreads.items():
        noise = np.random.default_rng([zlib.crc32(name.encode()), seed]).standard_normal(out[name].shape)
        drawn = base * np.exp(spread * noise) if base else spread * noise
        out[name] = jnp.asarray(drawn.astype(out[name].dtype))
    for name, factor in factors.items():
        out[name] = (out[name] * factor).astype(out[name].dtype)
    return out
```

```python
import concourse.bass as bass
from concourse import mybir
from contextlib import ExitStack

F32 = mybir.dt.float32
F16 = mybir.dt.float16
BF16 = mybir.dt.bfloat16
I32 = mybir.dt.int32
U32 = mybir.dt.uint32
ALU = mybir.AluOpType
ACT = mybir.ActivationFunctionType
AX_X = mybir.AxisListType.X

P = 128
NB = 32
H = 16
DK = P // H
HG = 4
HU = H // 2
E = 8
FF = 512
FC = FF // P
T = NB * P
GB = 4
NG = NB // GB
GT = GB * P
EPS = 1e-5
WSCALE = 64.0
TW = 256


def build(nc, a, out):
    with ExitStack() as ctx:
        def sb(name, shape, dt=F32):
            return ctx.enter_context(nc.sbuf_tensor(name, shape, dt))

        def sem(name):
            return ctx.enter_context(nc.semaphore(name))

        x = sb("x", [P, NB, P])
        stage = sb("stage", [P, 2048])
        ctxT = sb("ctxT", [P, 2, GT])
        qc = sb("qc", [P, HG, T], F16)
        kc = sb("kc", [P, HG, T], F16)
        xnh = qc[:, 0, :]
        xnl = qc[:, 1, :]
        v1 = sb("v1", [P, NB, H, DK + 1])
        kexp = sb("kexp", [P, 2, HG, 4, P], F16)
        wgh = sb("wgh", [P, E, FF], F16)
        wgl = sb("wgl", [P, E, FF], F16)
        wuh = sb("wuh", [P, E, FF], F16)
        wul = sb("wul", [P, E, FF], F16)
        wd = sb("wd", [P, E, FC, P])
        wq = sb("wq", [P, P])
        wk = sb("wk", [P, P])
        wv = sb("wv", [P, P])
        wo = sb("wo", [P, P])
        bias = sb("bias", [P, 4])
        bqs = sb("bqs", [P, 1])
        boe = sb("boe", [P, 1])
        bob = sb("bob", [P, P])
        gate = sb("gate", [P, E])
        identf = sb("identf", [P, P])
        maskf = sb("maskf", [P, P])
        identb = sb("identb", [P, P], BF16)
        mask4 = sb("mask4", [P, 4, P], BF16)
        sel8 = sb("sel8", [P, HU, P], BF16)
        stackq = sb("stackq", [P, 2, HG, P], F16)
        stackk = sb("stackk", [P, 2, HG, P], F16)
        ones = sb("ones", [P, P])
        stats = sb("stats", [P, NB, 6])
        mv = sb("mv", [P, NB, 2])
        rstd = sb("rstd", [P, NB])
        sd = sb("sd", [P, NB])
        nr = sb("nr", [P, NB])
        eps = sb("eps", [P, 1])
        xn = sb("xn", [P, GB, P])
        xnT = sb("xnT", [P, GT])
        hi = sb("hi", [P, 2, GT], F16)
        lo = sb("lo", [P, 2, GT], F16)
        negm = sb("negm", [P, 2, HU])
        negmT = sb("negmT", [P, P], BF16)
        pr = sb("pr", [P, 2, HU, P])
        prT = sb("prT", [P, 2, HU, P])
        stackf = pr[:, 0].rearrange("p (a g) m -> p a g m", a=2)
        stackkf = pr[:, 1].rearrange("p (a g) m -> p a g m", a=2)
        hid = prT[:].rearrange("p a (b c d) k -> p (a b) c (d k)", b=2, c=2)
        after = v1[:].rearrange("p b h d -> p (b h d)")
        logits = after[:, 0:256].rearrange("p (b e) -> p b e", b=NB)
        top = after[:, 256:512].rearrange("p (b e) -> p b e", b=NB)
        topi = after[:, 512:768].bitcast(U32).rearrange("p (b e) -> p b e", b=NB)
        hot = after[:, 768:1280].rearrange("p (k b e) -> p k b e", k=2, b=NB)
        comb = after[:, 1280:1536].rearrange("p (b e) -> p b e", b=NB)
        topf = after[:, 2560:2624].rearrange("p (k b) -> p k b", k=2)
        pw = after[:, 2624:2752].rearrange("p (k b) -> p k b", k=4)
        sg = after[:, 1536:2560].rearrange("p (n c) -> p n c", n=2)
        rsum = sb("rsum", [P, 2, HU])
        o = sb("o", [P, 2, P])
        oT = sb("oT", [P, P])
        iotae = sb("iotae", [P, E])

        S = ctx.enter_context(nc.psum_tensor("S", [P, 4, 512], F32))
        PT = ctx.enter_context(nc.psum_tensor("PT", [P, 2, 512], F32))
        M0 = ctx.enter_context(nc.psum_tensor("M0", [P, 512], F32))
        M1 = ctx.enter_context(nc.psum_tensor("M1", [P, 512], F32))

        (s_w, s_c, s_x, s_ctx_unused, s_set, s_setp, s_setq, s_wraw, s_wd, s_wsc, s_wconv, s_free) = [sem(n) for n in (
            "weights_in", "consts_in", "x_in", "ctx_in", "setup_dve", "setup_pe", "setup_pool",
            "ffn_raw_in", "wd_in", "ffn_scaled", "ffn_split", "stage_free")]
        (s_st, s_xn, s_xnT, s_xnTc, s_kv, s_q, s_hi, s_lo, s_v, s_stk, s_stka, s_stkv) = [sem(n) for n in (
            "ln_chain", "xn_ready", "xnT_psum", "xnT_copied", "kv_psum", "q_psum", "hi_ready", "lo_ready",
            "v_ready", "stacked_psum", "stacked_act", "stacked_dve")]
        (s_kx, s_sc, s_nm, s_mT, s_mTc, s_sh, s_pr, s_pT, s_pTa, s_pTv, s_pv, s_rs, s_no, s_oT, s_oTc, s_pj,
         s_x2) = [sem(n) for n in (
            "kexp_ready", "scores_psum", "negmax_ready", "maxT_psum", "maxT_copied", "shifted", "probs_ready",
            "probsT_psum", "probsT_act", "probsT_dve", "pv_psum", "rsum_ready", "attn_normed", "oT_psum",
            "oT_copied", "proj_psum", "x2_ready")]
        s_rs2 = sem("x_plus_bias")
        s_rt = sem("root_ready")
        s_ctx = [sem("ctx_in_0"), sem("ctx_in_1")]
        (s_st2, s_xn2, s_t2, s_h2, s_f2, s_l2, s_lg, s_lgc, s_tp, s_ex, s_cm) = [sem(n) for n in (
            "ln2_chain", "xn2_ready", "xn2T_psum", "xn2_high", "xn2T_copied", "xn2_low", "logits_psum",
            "logits_copied", "top_chain", "top_exp", "combine_ready")]
        (s_g, s_u, s_sg, s_h, s_y, s_acc, s_out) = [sem(n) for n in (
            "gate_psum", "up_psum", "silu_ready", "hidden_ready", "y_psum", "acc_done", "out_stored")]

        xf = a["x"].rearrange("b s d -> s b d")
        of = out.rearrange("b s d -> s b d")
        block = ctx.enter_context(nc.Block())

        SCORE_SCALE = float(DK) ** -0.5

        @block.sync
        def _(sp):
            for t, n in ((wq, "wqT"), (wk, "wkT"), (wv, "wvT"), (wo, "woT"), (bias, "bias"), (gate, "gateT")):
                sp.dma_start(t[:], a[n]).then_inc(s_w, 16)
            for t, n in ((identf, "ident"), (maskf, "mask"), (iotae, "iotae")):
                sp.dma_start(t[:], a[n]).then_inc(s_c, 16)
            sp.dma_start(stackf.rearrange("p a g m -> p (a g m)"), a["stackq"]).then_inc(s_c, 16)
            sp.dma_start(stackkf.rearrange("p a g m -> p (a g m)"), a["stackk"]).then_inc(s_c, 16)
            for i in range(4):
                sp.dma_start(x[:, 8 * i:8 * i + 8, :], xf[:, 8 * i:8 * i + 8, :]).then_inc(s_x, 16)
                if i < 2:
                    sp.dma_start(ctxT[:, i, :], a["ctxT"][:, i * GT:(i + 1) * GT]).then_inc(s_ctx[i], 16)
            sp.dma_start(stage[:], a["wgT"][:, 0:2048]).then_inc(s_wraw, 16)
            sp.dma_start(wd[:].rearrange("p e c d -> p (e c d)"), a["wdT"]).then_inc(s_wd, 16)
            with sp.Fori(1, NG // 2) as h:
                for k in range(2):
                    sp.wait_ge(s_kv, h * 2 + (k - 1))
                    sp.dma_start(ctxT[:, k, :], a["ctxT"][:, bass.ds(h * (2 * GT) + k * GT, GT)]).then_inc(s_ctx[k], 16)
            for i in range(1, 4):
                sp.wait_ge(s_wconv, i)
                sp.dma_start(stage[:], a["wgT" if i < 2 else "wuT"][:, (i % 2) * 2048:(i % 2) * 2048 + 2048]).then_inc(s_wraw, 16)
            with sp.Fori(0, NB // 2) as g:
                sp.wait_ge(s_acc, (g + 1) * (2 * E))
                sp.dma_start(of[:, bass.ds(g * 2, 2), :], x[:, bass.ds(g * 2, 2), :]).then_inc(s_out, 16)
            sp.wait_ge(s_out, 16 * (NB // 2))

        @block.gpsimd
        def _(pool):
            pool.memset(kexp[:], 0.0).then_inc(s_setq, 1)
            pool.memset(negmT[:], 0.0).then_inc(s_setq, 1)
            pool.memset(v1[:], 1.0).then_inc(s_setq, 1)
            pool.memset(eps[:], EPS)
            pool.memset(ones[:], 1.0).then_inc(s_setq, 1)

            for w in range(4):
                hi_w, lo_w = (t[:, 4 * (w % 2):4 * (w % 2) + 4, :] for t in ((wgh, wgl) if w < 2 else (wuh, wul)))
                pool.wait_ge(s_wraw, 16 * (w + 1))
                st = stage[:].rearrange("p (e f) -> p e f", e=E // 2)
                pool.tensor_scalar(st, st, WSCALE, None, ALU.mult).then_inc(s_wsc, 1)
                pool.wait_ge(s_wsc, 3 * w + 1)
                pool.tensor_copy(hi_w, st).then_inc(s_wsc, 1)
                pool.wait_ge(s_wsc, 3 * w + 2)
                pool.tensor_tensor(lo_w, st, hi_w, ALU.subtract).then_inc(s_wsc, 1)
                pool.wait_ge(s_wsc, 3 * w + 3)
                pool.sem_inc(s_wconv, 1)

            def expand(b, par):
                for s in range(4):
                    ins = pool.tensor_copy(kexp[32 * s:32 * s + 32, par, :, s, :],
                                           kc[32 * s:32 * s + 32, :, bass.ds(b * P, P)])
                ins.then_inc(s_kx, 1)

            pool.wait_ge(s_setq, 4)
            pool.wait_ge(s_stka, 4 * NG)
            pool.wait_ge(s_stkv, 4 * NG)
            expand(0, 0)
            expand(1, 1)
            with pool.Fori(1, NB // 2) as h:
                pool.wait_ge(s_sc, h * 4 - 2)
                expand(h * 2, 0)
                pool.wait_ge(s_sc, h * 4)
                expand(h * 2 + 1, 1)

        @block.tensor
        def _(pe):
            pe.wait_ge(s_w, 96)
            pe.wait_ge(s_set, 1)
            pe.matmul(M0[:, 0:P], bob[:], wo[:], start=True, stop=True).then_inc(s_setp, 1)
            pe.wait_ge(s_c, 80)
            pe.wait_ge(s_set, 2)
            pe.wait_ge(s_setq, 4)
            pe.matmul(M0[:, 0:P], ones[:], maskf[:], start=True, stop=True).then_inc(s_setp, 1)

            pe.wait_ge(s_set, 3)

            def project(i, h, k):
                pe.wait_ge(s_ctx[k], h * 16 + 16)
                pe.wait_ge(s_lo, i * 2)
                pe.matmul(M0[:], wk[:], ctxT[:, k, :], start=True, stop=True)
                pe.wait_ge(s_v, i)
                for j in range(GB):
                    mm = pe.matmul(M1[:, j * P:j * P + P], ctxT[:, k, j * P:j * P + P], wv[:],
                                   start=True, stop=True)
                mm.then_inc(s_kv, 1)
                pe.wait_ge(s_xn, i + 1)
                pe.wait_ge(s_xnTc, i)
                for j in range(GB):
                    mm = pe.transpose(PT[:, 0, j * P:j * P + P], xn[:, j, :], identf[:])
                mm.then_inc(s_xnT, 1)
                pe.wait_ge(s_xnTc, i + 1)
                pe.matmul(PT[:, 1, :], wq[:], xnT[:], start=True, stop=True).then_inc(s_q, 1)
                for w, st in ((0, stackk), (1, stackq)):
                    pe.wait_ge(s_lo, i * 2 + w + 1)
                    for g in range(HG):
                        drained = s_stka if g % 2 == 0 else s_stkv
                        pe.wait_ge(drained, i * 4 if w == 0 else i * 4 + g // 2 + 1)
                        pe.matmul(S[:, g, :], st[:, 0, g, :], hi[:, w, :], start=True, stop=False)
                        pe.matmul(S[:, g, :], st[:, 1, g, :], lo[:, w, :], start=False, stop=True).then_inc(s_stk, 1)

            with pe.Fori(0, NG // 2) as h:
                project(h * 2, h, 0)
                project(h * 2 + 1, h, 1)

            pe.wait_ge(s_stka, 4 * NG)
            pe.wait_ge(s_stkv, 4 * NG)
            pe.wait_ge(s_v, NG)

            def scores(b, g, u, first=False):
                if g == 0:
                    pe.wait_ge(s_kx, b + 1)
                if not first:
                    pe.wait_ge(s_pr, u - 1)
                for k in range(2):
                    hg = 2 * g + k
                    bank = S[:, 2 * g + k, :]
                    pe.matmul(bank, identb[:], mask4[:].rearrange("p h k -> p (h k)"), start=True, stop=False)
                    mm = pe.matmul(bank, qc[:, hg, bass.ds(b * P, P)],
                                   kexp[:, pa(b), hg, :, :].rearrange("p s k -> p (s k)"), start=False, stop=True)
                mm.then_inc(s_sc, 1)

            par = [0]

            def pa(b):
                return par[0]

            def shift(g, u, first):
                pe.wait_ge(s_nm, u + 1)
                if not first:
                    pe.wait_ge(s_no, u - 2)
                pe.transpose(M1[0:HU, 256:256 + P], negm[:, g, :], identf[:]).then_inc(s_mT, 1)
                pe.wait_ge(s_mTc, u + 1)
                for k in range(2):
                    mm = pe.matmul(S[:, 2 * g + k, :], negmT[:],
                                   sel8[:, 4 * k:4 * k + 4, :].rearrange("p h k -> p (h k)"),
                                   start=False, stop=True, skip_group_check=True)
                mm.then_inc(s_sh, 1)

            def turn(g, u, first):
                pe.wait_ge(s_pr, u + 1)
                for k in range(2):
                    if not first:
                        pe.wait_ge(s_pTa if k == 0 else s_pTv, u)
                    for h in range(4):
                        mm = pe.transpose(PT[:, k, h * P:h * P + P], pr[:, g, 4 * k + h, :], identf[:])
                    mm.then_inc(s_pT, 1)

            def pv(b, g, u, ahead):
                pe.wait_ge(s_pTa, u + 1)
                pe.wait_ge(s_pTv, u + 1)
                pe.wait_ge(s_mTc, ahead)
                if not (isinstance(u, int) and u == 0):
                    pe.wait_ge(s_no, u)
                for h in range(HU):
                    mm = pe.matmul(M1[:, h * (DK + 1):(h + 1) * (DK + 1)], prT[:, g, h, :],
                                   v1[:, bass.ds(b, 1), HU * g + h, :].rearrange("p a d -> p (a d)"),
                                   start=True, stop=True)
                mm.then_inc(s_pv, 1)

            def out_turn(b, par2, first):
                pe.wait_ge(s_no, b * 2 + 2)
                if not first:
                    pe.wait_ge(s_x2, b)
                pe.transpose(M0[:, 0:P], o[:, par2, :], identf[:]).then_inc(s_oT, 1)

            def out_proj(b):
                pe.wait_ge(s_oTc, b + 1)
                pe.matmul(M0[:, P:2 * P], oT[:], wo[:], start=True, stop=True).then_inc(s_pj, 1)

            def batch(b, parity, n):
                known = n is not None
                for g in range(2):
                    u = b * 2 + g
                    if not known or n < NB:
                        shift(g, u, known and 2 * n + g < 3)
                        if g == 0:
                            par[0] = parity
                            scores(b, 1, u + 1, known and 2 * n + 1 < 2)
                        elif not known or n < NB - 1:
                            par[0] = 1 - parity
                            scores(b + 1, 0, u + 1, known and 2 * n + 2 < 2)
                    if not known or 0 <= 2 * n + g - 1 < 2 * NB:
                        turn(1 - g, u - 1, known and 2 * n + g - 1 < 1)
                    if not known or 0 <= 2 * n + g - 2 < 2 * NB:
                        pv(b - 1, g, u - 2, u + 1 if not known else min(2 * n + g + 1, 2 * NB))
                    if not known or 0 <= n - 2 < NB:
                        if g == 0:
                            out_turn(b - 2, parity, known and n == 2)
                        else:
                            out_proj(b - 2)

            par[0] = 0
            scores(0, 0, 0, True)
            batch(0, 0, 0)
            batch(1, 1, 1)
            batch(2, 0, 2)
            batch(3, 1, 3)
            with pe.Fori(2, NB // 2 - 1) as h:
                batch(h * 2, 0, None)
                batch(h * 2 + 1, 1, None)
            for n in range(NB - 2, NB + 2):
                batch(n, n % 2, n)

            with pe.Fori(0, NG) as i:
                pe.wait_ge(s_xn2, i + 1)
                pe.wait_ge(s_l2, i)
                pe.wait_ge(s_f2, i)
                for j in range(GB):
                    mm = pe.transpose(PT[:, 0, j * P:j * P + P], xn[:, j, :], identf[:])
                mm.then_inc(s_t2, 1)
                pe.wait_ge(s_f2, i + 1)
                pe.wait_ge(s_lgc, i)
                for j in range(GB):
                    mm = pe.matmul(M1[:, j * E:j * E + E], xnT[:, j * P:j * P + P], gate[:], start=True, stop=True)
                mm.then_inc(s_lg, 1)
            pe.wait_ge(s_lgc, NG)
            pe.wait_ge(s_l2, NG)
            pe.wait_ge(s_wconv, 4)
            pe.wait_ge(s_wd, 16)

            with pe.Fori(0, T // TW) as tg:
                def gate_up(e):
                    for hf in range(2):
                        n = tg * (2 * E) + 2 * e + hf
                        for (ps, wh, wl, free, done) in ((S[:, hf, :], wgh, wgl, s_sg, s_g),
                                                         (S[:, 2 + hf, :], wuh, wul, s_h, s_u)):
                            if e == 0:
                                pe.wait_ge(free, tg * (2 * E))
                            else:
                                pe.wait_ge(free, n - 1)
                            for c in range(2):
                                col = (2 * hf + c) * P
                                dst = ps[:, c * TW:c * TW + TW]
                                xh_t = xnh[:, bass.ds(tg * TW, TW)]
                                xl_t = xnl[:, bass.ds(tg * TW, TW)]
                                pe.matmul(dst, wh[:, e, col:col + P], xh_t, start=True, stop=False)
                                pe.matmul(dst, wh[:, e, col:col + P], xl_t, start=False, stop=False)
                                mm = pe.matmul(dst, wl[:, e, col:col + P], xh_t, start=False, stop=True)
                            mm.then_inc(done, 1)

                def down(e):
                    pe.wait_ge(s_h, tg * (2 * E) + 2 * e + 2)
                    if e >= 2:
                        pe.wait_ge(s_acc, tg * (2 * E) + 2 * e - 2)
                    else:
                        pe.wait_ge(s_acc, tg * (2 * E))
                    for th in range(2):
                        for c in range(FC):
                            mm = pe.matmul(PT[:, e % 2, th * P:th * P + P],
                                           hid[:, 2 * (e % 2) + c // 2, c % 2, th * P:th * P + P],
                                           wd[:, e, c, :], start=(c == 0), stop=(c == FC - 1))
                    mm.then_inc(s_y, 1)

                for e in range(E):
                    gate_up(e)
                    if e:
                        down(e - 1)
                down(E - 1)

        @block.scalar
        def _(act):
            act.wait_ge(s_set, 3)

            def roots(chain, aggregated):
                act.wait_ge(chain, aggregated)
                act.activation(sd[:], mv[:, :, 1], ACT.Sqrt, bias=eps[:, 0:1]).then_inc(s_rt, 1)

            roots(s_st, 2 + NG)
            with act.Fori(0, NG) as i:
                act.wait_ge(s_kv, i + 1)
                act.activation(hi[:, 0, :], M0[:], ACT.Identity, bias=bias[:, 1:2]).then_inc(s_hi, 1)
                act.wait_ge(s_setq, 4)
                act.activation(v1[:, bass.ds(i * GB, GB), :, 0:DK],
                               M1[:].rearrange("p (b h d) -> p b h d", b=GB, h=H), ACT.Identity).then_inc(s_v, 1)
                act.wait_ge(s_xnT, i + 1)
                act.activation(xnT[:], PT[:, 0, :], ACT.Identity).then_inc(s_xnTc, 1)
                act.wait_ge(s_q, i + 1)
                act.activation(hi[:, 1, :], PT[:, 1, :], ACT.Identity, bias=bqs[:, 0:1]).then_inc(s_hi, 1)
                for w, dst in ((0, kc), (1, qc)):
                    for g in (0, 2):
                        act.wait_ge(s_stk, i * 8 + 4 * w + g + 1)
                        act.activation(dst[:, g, bass.ds(i * GT, GT)], S[:, g, :], ACT.Identity).then_inc(s_stka, 1)

            def exps(g, u, first):
                act.wait_ge(s_sh, u + 1)
                if not first:
                    act.wait_ge(s_pT, u * 2 - 2)
                act.activation(pr[:, g, :, :].rearrange("p (k h) c -> p k (h c)", k=2), S[:, 2 * g:2 * g + 2, :],
                               ACT.Exp).then_inc(s_pr, 1)

            def turned(g, u, first):
                act.wait_ge(s_pT, u * 2 + 1)
                if not first:
                    act.wait_ge(s_pv, u - 1)
                act.activation(prT[:, g, 0:4, :].rearrange("p h q -> p (h q)"), PT[:, 0, :],
                               ACT.Identity).then_inc(s_pTa, 1)

            def batch(b, n):
                known = n is not None
                for g in range(2):
                    u = b * 2 + g
                    if not known or n < NB:
                        exps(g, u, known and 2 * n + g < 2)
                    if not known or 0 <= 2 * n + g - 1 < 2 * NB:
                        turned(1 - g, u - 1, known and 2 * n + g - 1 < 2)
                    if g == 0 and (not known or 0 <= n - 2 < NB):
                        act.wait_ge(s_oT, b - 1)
                        act.activation(oT[:], M0[:, 0:P], ACT.Identity).then_inc(s_oTc, 1)

            for n in range(3):
                batch(n, n)
            with act.Fori(3, NB) as b:
                batch(b, None)
            batch(NB, NB)
            batch(NB + 1, NB + 1)

            roots(s_st2, 1 + NG)
            with act.Fori(0, NG) as i:
                act.wait_ge(s_t2, i + 1)
                act.activation(xnh[:, bass.ds(i * GT, GT)], PT[:, 0, :], ACT.Identity).then_inc(s_h2, 1)
                act.wait_ge(s_lg, i)
                act.activation(xnT[:], PT[:, 0, :], ACT.Identity).then_inc(s_f2, 1)
            act.wait_ge(s_tp, 3)
            act.activation(pw[:, 1, :], pw[:, 0, :], ACT.Exp).then_inc(s_ex, 1)

            with act.Fori(0, T // TW) as tg:
                for n in range(2 * E):
                    m = tg * (2 * E) + n
                    act.wait_ge(s_g, m + 1)
                    if n >= 2:
                        act.wait_ge(s_h, m - 1)
                    else:
                        act.wait_ge(s_h, tg * (2 * E))
                    act.activation(sg[:, n % 2, :], S[:, n % 2, :], ACT.Silu, scale=1.0 / WSCALE).then_inc(s_sg, 1)

        @block.vector
        def _(dve):
            dve.wait_ge(s_w, 96)
            dve.wait_ge(s_c, 80)
            dve.wait_ge(s_setq, 4)
            dve.tensor_scalar(bob[:], ones[:], bias[:, 2:3], None, ALU.mult).then_inc(s_set, 1)
            dve.tensor_copy(identb[:], identf[:])
            for h in range(4):
                dve.tensor_copy(mask4[:, h, :], maskf[:])
            dve.tensor_copy(stackq[:], stackf)
            dve.tensor_copy(stackk[:], stackkf)
            for h in range(HU):
                dve.tensor_scalar(sel8[:, h, :], ones[:], identf[:, h:h + 1], None, ALU.mult)
            dve.tensor_scalar(bqs[:], bias[:, 0:1], SCORE_SCALE, None, ALU.mult)
            dve.tensor_scalar(wq[:], wq[:], SCORE_SCALE, None, ALU.mult).then_inc(s_st, 1)
            dve.wait_ge(s_st, 1)
            dve.wait_ge(s_setp, 1)
            dve.tensor_copy(bob[:], M0[:, 0:P])
            dve.tensor_scalar(maskf[:], identf[:], bias[:, 3:4], None, ALU.mult).then_inc(s_set, 1)
            dve.wait_ge(s_setp, 2)
            dve.wait_ge(s_set, 2)
            dve.tensor_tensor(bob[:], M0[:, 0:P], bob[:], ALU.add).then_inc(s_set, 1)

            def ln_stats(chain, base, root):
                with dve.Fori(0, NG) as i:
                    for j in range(GB):
                        b = i * GB + j
                        ins = dve.bn_stats(stats[:, bass.ds(b, 1), :].rearrange("p a d -> p (a d)"),
                                           x[:, bass.ds(b, 1), :].rearrange("p a d -> p (a d)"))
                    ins.then_inc(chain, 1)
                dve.wait_ge(chain, base + NG)
                for b in range(NB):
                    ins = dve.bn_aggr(mv[:, b, :], stats[:, b, :])
                ins.then_inc(chain, 1)
                n = base + NG + 1
                dve.wait_ge(chain, n)
                dve.tensor_scalar(nr[:], mv[:, :, 1], EPS, None, ALU.add).then_inc(chain, 1)
                dve.wait_ge(root, 1 if base else 2)
                dve.reciprocal(rstd[:], sd[:]).then_inc(chain, 1)
                dve.wait_ge(chain, n + 2)
                dve.tensor_tensor(nr[:], nr[:], rstd[:], ALU.mult).then_inc(chain, 1)
                dve.wait_ge(chain, n + 3)
                dve.tensor_tensor(nr[:], nr[:], rstd[:], ALU.mult).then_inc(chain, 1)
                dve.wait_ge(chain, n + 4)
                dve.tensor_scalar(nr[:], nr[:], -0.5, 1.5, ALU.mult, ALU.add).then_inc(chain, 1)
                dve.wait_ge(chain, n + 5)
                dve.tensor_tensor(rstd[:], rstd[:], nr[:], ALU.mult).then_inc(chain, 1)
                dve.wait_ge(chain, n + 6)

            def layer_norm(i, ready, guard):
                dve.wait_ge(guard, i)
                for j in range(GB):
                    ins = dve.tensor_scalar(xn[:, j, :], x[:, bass.ds(i * GB + j, 1), :].rearrange("p a d -> p (a d)"),
                                            mv[:, bass.ds(i * GB + j, 1), 0], rstd[:, bass.ds(i * GB + j, 1)],
                                            ALU.subtract, ALU.mult)
                ins.then_inc(ready, 1)

            dve.wait_ge(s_x, 64)
            ln_stats(s_st, 1, s_rt)
            with dve.Fori(0, NG) as i:
                layer_norm(i, s_xn, s_xnT)
                dve.wait_ge(s_hi, i * 2 + 1)
                dve.scalar_tensor_tensor(lo[:, 0, :], M0[:], bias[:, 1:2], hi[:, 0, :], ALU.add, ALU.subtract).then_inc(s_lo, 1)
                dve.wait_ge(s_hi, i * 2 + 2)
                dve.scalar_tensor_tensor(lo[:, 1, :], PT[:, 1, :], bqs[:, 0:1], hi[:, 1, :], ALU.add, ALU.subtract).then_inc(s_lo, 1)
                for w, dst in ((0, kc), (1, qc)):
                    for g in (1, 3):
                        dve.wait_ge(s_stk, i * 8 + 4 * w + g + 1)
                        dve.tensor_copy(dst[:, g, bass.ds(i * GT, GT)], S[:, g, :]).then_inc(s_stkv, 1)

            def maxima(g, u):
                dve.wait_ge(s_sc, u + 1)
                dve.tensor_reduce(negm[:, g, :], S[:, 2 * g:2 * g + 2, :].rearrange("p k (h c) -> p (k h) c", h=4),
                                  AX_X, ALU.max, negate=True).then_inc(s_nm, 1)

            def norm(g, b2, u):
                dve.wait_ge(s_pv, u + 1)
                acc = M1[:, 0:HU * (DK + 1)].rearrange("p (h d) -> p h d", h=HU)
                dve.reciprocal(rsum[:, g, :], acc[:, :, DK]).then_inc(s_rs, 1)
                dve.wait_ge(s_rs, u + 1)
                dve.tensor_tensor(o[:, b2, g * 64:g * 64 + 64].rearrange("p (h d) -> p h d", h=HU), acc[:, :, 0:DK],
                                  rsum[:, g, :].unsqueeze(2).to_broadcast([P, HU, DK]), ALU.mult).then_inc(s_no, 1)

            def batch(b, parity, n):
                known = n is not None
                for g in range(2):
                    u = b * 2 + g
                    if not known or n < NB:
                        dve.wait_ge(s_mT, u + 1)
                        if not (known and 2 * n + g == 0):
                            dve.wait_ge(s_sh, u)
                        dve.tensor_copy(negmT[0:HU, :], M1[0:HU, 256:256 + P]).then_inc(s_mTc, 1)
                        if not (known and n == NB - 1 and g == 1):
                            maxima(1 - g, u + 1)
                    if not known or 0 <= 2 * n + g - 1 < 2 * NB:
                        dve.wait_ge(s_pT, u * 2)
                        if not known or 2 * n + g - 1 >= 2:
                            dve.wait_ge(s_pv, u - 2)
                        dve.tensor_copy(prT[:, 1 - g, 4:8, :].rearrange("p h q -> p (h q)"), PT[:, 1, :]).then_inc(s_pTv, 1)
                    if not known or 0 <= 2 * n + g - 2 < 2 * NB:
                        if not known or n - 1 >= 2:
                            dve.wait_ge(s_oT, b - 2)
                        norm(g, 1 - parity, u - 2)
                    if g == 1 and (not known or 0 <= n - 2 < NB):
                        dve.wait_ge(s_pj, b - 1)
                        xb = x[:, bass.ds(b - 2, 1), :].rearrange("p a d -> p (a d)")
                        dve.tensor_tensor(xb, xb, bob[:], ALU.add).then_inc(s_rs2, 1)
                        dve.wait_ge(s_rs2, b - 1)
                        dve.tensor_tensor(xb, M0[:, P:2 * P], xb, ALU.add).then_inc(s_x2, 1)

            maxima(0, 0)
            for n in range(4):
                batch(n, n % 2, n)
            with dve.Fori(2, NB // 2 - 1) as h:
                batch(h * 2, 0, None)
                batch(h * 2 + 1, 1, None)
            for n in range(NB - 2, NB + 2):
                batch(n, n % 2, n)
            dve.wait_ge(s_x2, NB)

            ln_stats(s_st2, 0, s_rt)
            with dve.Fori(0, NG) as i:
                layer_norm(i, s_xn2, s_t2)
                dve.wait_ge(s_h2, i + 1)
                dve.wait_ge(s_f2, i + 1)
                dve.tensor_tensor(xnl[:, bass.ds(i * GT, GT)], PT[:, 0, :], xnh[:, bass.ds(i * GT, GT)], ALU.subtract).then_inc(s_l2, 1)
                dve.wait_ge(s_lg, i + 1)
                dve.tensor_copy(logits[:, bass.ds(i * GB, GB), :], M1[:, 0:GB * E].rearrange("p (b e) -> p b e", b=GB)).then_inc(s_lgc, 1)
            dve.wait_ge(s_lgc, NG)
            for t in range(NB):
                ins = dve.max(top[:, t, :], logits[:, t, :])
            ins.then_inc(s_tp, 1)
            dve.wait_ge(s_tp, 1)
            for t in range(NB):
                ins = dve.max_index(topi[:, t, :], top[:, t, :], logits[:, t, :])
            ins.then_inc(s_tp, 1)
            dve.wait_ge(s_tp, 2)
            dve.tensor_copy(topf.rearrange("p k t -> p t k"), topi[:, :, 0:2])
            dve.tensor_tensor(pw[:, 0, :], top[:, :, 1], top[:, :, 0], ALU.subtract).then_inc(s_tp, 1)
            dve.wait_ge(s_ex, 1)
            dve.tensor_scalar(pw[:, 2, :], pw[:, 1, :], 1.0, None, ALU.add).then_inc(s_tp, 1)
            dve.wait_ge(s_tp, 4)
            dve.reciprocal(pw[:, 3, :], pw[:, 2, :]).then_inc(s_tp, 1)
            dve.wait_ge(s_tp, 5)
            dve.tensor_tensor(pw[:, 0, :], pw[:, 3, :], pw[:, 1, :], ALU.mult).then_inc(s_tp, 1)
            dve.wait_ge(s_tp, 6)
            for k in range(2):
                dve.tensor_tensor(hot[:, k], topf[:, k, :].unsqueeze(2).to_broadcast([P, NB, E]),
                                  iotae[:].unsqueeze(1).to_broadcast([P, NB, E]), ALU.is_equal).then_inc(s_tp, 1)
            for k in range(2):
                dve.wait_ge(s_tp, 7 + k)
                dve.tensor_tensor(hot[:, k], hot[:, k], pw[:, 3 if k == 0 else 0, :].unsqueeze(2).to_broadcast([P, NB, E]),
                                  ALU.mult).then_inc(s_tp, 1)
            dve.wait_ge(s_tp, 10)
            dve.tensor_tensor(comb, hot[:, 0], hot[:, 1], ALU.add).then_inc(s_cm, 1)
            dve.wait_ge(s_cm, 1)

            with dve.Fori(0, T // TW) as tg:
                def combine(e):
                    dve.wait_ge(s_y, tg * E + e + 1)
                    dve.wait_ge(s_acc, tg * (2 * E) + 2 * e)
                    for th in range(2):
                        xb = x[:, bass.ds(tg * 2 + th, 1), :].rearrange("p a d -> p (a d)")
                        dve.scalar_tensor_tensor(xb, PT[:, e % 2, th * P:th * P + P],
                                                 comb[:, bass.ds(tg * 2 + th, 1), e], xb, ALU.mult, ALU.add).then_inc(s_acc, 1)

                for e in range(E):
                    for hf in range(2):
                        m = tg * (2 * E) + 2 * e + hf
                        dve.wait_ge(s_sg, m + 1)
                        dve.wait_ge(s_u, m + 1)
                        if e >= 2:
                            dve.wait_ge(s_y, tg * E + e - 1)
                        else:
                            dve.wait_ge(s_y, tg * E)
                        dve.scalar_tensor_tensor(hid[:, 2 * (e % 2) + hf, :, :].rearrange("p c t -> p (c t)"), S[:, 2 + hf, :],
                                                 1.0 / WSCALE, sg[:, hf, :], ALU.mult, ALU.mult).then_inc(s_h, 1)
                    if e:
                        combine(e - 1)
                combine(E - 1)


_NAMES = ["x", "ctxT", "wqT", "wkT", "wvT", "woT", "bias", "gateT", "wgT", "wuT", "wdT",
          "ident", "mask", "iotae", "stackq", "stackk"]


def kernel(x, ctx_1024, L0_xattn_w_q, L0_xattn_b_q, L0_xattn_w_k, L0_xattn_b_k, L0_xattn_w_v, L0_xattn_b_v,
           L0_xattn_w_o, L0_xattn_b_o, L0_ffn_gate_w, L0_ffn_wg, L0_ffn_wu, L0_ffn_wd):
    import numpy as np
    import concourse.bacc as bacc
    from concourse.bass_utils import run_bass_kernel_spmd

    c = np.ascontiguousarray
    stack = np.zeros((2, P, 2, HG, P), np.float32)
    for h in range(H):
        g, s = h // 4, h % 4
        for d in range(DK):
            for t in range(4):
                stack[0, h * DK + d, t // 2, g, 32 * s + DK * t + d] = 1.0
                stack[1, h * DK + d, t % 2, g, 32 * s + DK * t + d] = 1.0
    r = np.arange(P)
    arrays = {
        "x": c(x),
        "ctxT": c(np.asarray(ctx_1024).reshape(T, P).T),
        "wqT": c(np.asarray(L0_xattn_w_q).T), "wkT": c(np.asarray(L0_xattn_w_k).T),
        "wvT": c(np.asarray(L0_xattn_w_v).T), "woT": c(np.asarray(L0_xattn_w_o).T),
        "bias": c(np.stack([np.asarray(v) for v in (L0_xattn_b_q, L0_xattn_b_k, L0_xattn_b_v, L0_xattn_b_o)], 1)),
        "gateT": c(np.asarray(L0_ffn_gate_w).T),
        "wgT": c(np.asarray(L0_ffn_wg).transpose(2, 0, 1).reshape(P, E * FF)),
        "wuT": c(np.asarray(L0_ffn_wu).transpose(2, 0, 1).reshape(P, E * FF)),
        "wdT": c(np.asarray(L0_ffn_wd).transpose(2, 0, 1).reshape(FC, P, E, P).transpose(1, 2, 0, 3).reshape(P, E * FC * P)),
        "ident": np.eye(P, dtype=np.float32),
        "mask": np.where(r[None, :] <= r[:, None], 0.0, -1e30).astype(np.float32),
        "iotae": c(np.broadcast_to(np.arange(E, dtype=np.float32), (P, E))),
        "stackq": c(stack[0].reshape(P, -1)), "stackk": c(stack[1].reshape(P, -1)),
    }
    nc = bacc.Bacc("TRN2", target_bir_lowering=False, num_devices=1)
    aps = {n: nc.dram_tensor(f"in_{n}", arrays[n].shape, mybir.dt.from_np(arrays[n].dtype), kind="ExternalInput").ap()
           for n in _NAMES}
    out = nc.dram_tensor("out_0", (NB, P, P), F32, kind="ExternalOutput").ap()
    build(nc, aps, out)
    res = run_bass_kernel_spmd(nc, [{f"in_{n}": arrays[n] for n in _NAMES}], core_ids=[0])
    return res.results[0]["out_0"]
```

```python
import concourse.bass as bass
from concourse import mybir
from contextlib import ExitStack

F32 = mybir.dt.float32
F16 = mybir.dt.float16
BF16 = mybir.dt.bfloat16
I32 = mybir.dt.int32
U32 = mybir.dt.uint32
ALU = mybir.AluOpType
ACT = mybir.ActivationFunctionType
AX_X = mybir.AxisListType.X

P = 128
NB = 32
H = 16
DK = P // H
HG = 4
HU = H // 2
E = 8
FF = 512
FC = FF // P
T = NB * P
GB = 4
NG = NB // GB
GT = GB * P
EPS = 1e-5
WSCALE = 64.0
TW = 256
NT = 2 * T // TW + E - 1
REG = T + TW
DUMP = E * REG
RW = P + 4
MAGIC = 0x5F3759DF
NPAIR = NB // 2


SM, SMALL = {}, 0
for _n, _w in (("iota", E), ("reg", E), ("tri", E * E), ("row", NT), ("tok", 2)):
    SM[_n] = (SMALL, SMALL + _w)
    SMALL += _w


def settle(eng, semaphore, count, spare):
    eng.wait_ge(semaphore, count)
    if not isinstance(count, int):
        eng.sem_inc(spare, 1)


def after(eng, semaphore, count):
    if not (isinstance(count, int) and count <= 0):
        eng.wait_ge(semaphore, count)


def on(n, low, high):
    return n is None or low <= n < high


def build(nc, a, out):
    with ExitStack() as ctx:
        def sb(name, shape, dt=F32):
            return ctx.enter_context(nc.sbuf_tensor(name, shape, dt))

        def sem(name):
            return ctx.enter_context(nc.semaphore(name))

        x = sb("x", [P, NB, P])
        qc = sb("qc", [P, HG, T], F16)
        kc = sb("kc", [P, HG, T], F16)
        v1 = sb("v1", [P, NB, H, DK + 1])
        kexp = sb("kexp", [P, 2, HG, 4, P], F16)
        wgh = sb("wgh", [P, E, FF], F16)
        wgl = sb("wgl", [P, E, FF], F16)
        wuh = sb("wuh", [P, E, FF], F16)
        wul = sb("wul", [P, E, FF], F16)
        wd = sb("wd", [P, E, FC, P])
        stage = sb("stage", [P, 1024])
        ctxT = sb("ctxT", [P, 2, GT])
        wq = sb("wq", [P, P])
        wk = sb("wk", [P, P])
        wv = sb("wv", [P, P])
        wo = sb("wo", [P, P])
        bias = sb("bias", [P, 4])
        bqs = sb("bqs", [P, 1])
        bob = sb("bob", [P, P])
        gate = sb("gate", [P, E])
        identf = sb("identf", [P, P])
        maskf = sb("maskf", [P, P])
        upperf = sb("upperf", [P, P])
        identb = sb("identb", [P, P], BF16)
        upperb = sb("upperb", [P, P], BF16)
        onesb = sb("onesb", [P, P], BF16)
        mask4 = sb("mask4", [P, 4, P], BF16)
        sel8 = sb("sel8", [P, HU, P], BF16)
        stackq = sb("stackq", [P, 2, HG, P], F16)
        stackk = sb("stackk", [P, 2, HG, P], F16)
        ones = sb("ones", [P, P])
        small = sb("small", [P, SMALL])
        stats = sb("stats", [P, NB, 6])
        mv = sb("mv", [P, NB, 2])
        rstd = sb("rstd", [P, NB])
        sd = sb("sd", [P, NB])
        nr = sb("nr", [P, NB])
        eps = sb("eps", [P, 1])
        xn = sb("xn", [P, GB, P])
        xnT = sb("xnT", [P, GT])
        hi = sb("hi", [P, 2, GT], F16)
        lo = sb("lo", [P, 2, GT], F16)
        negm = sb("negm", [P, 2, HU])
        negmT = sb("negmT", [P, P], BF16)
        pr = sb("pr", [P, 2, HU, P])
        prT = sb("prT", [P, 2, HU, P])
        rsum = sb("rsum", [P, 2, HU])
        rows = sb("rows", [P, 2, 2, 2, RW])
        seed = sb("seed", [P, 2])
        var2 = sb("var2", [P, 2])
        y2 = sb("y2", [P, 2])
        t2 = sb("t2", [P, 2])
        mv2 = sb("mv2", [P, 2, 2])
        st2 = sb("st2", [P, 2, 6])
        lg = sb("lg", [P, 2, E])
        top = sb("top", [P, 2, 8])
        topi = sb("topi", [P, 2, 8], U32)
        dif = sb("dif", [P, 2])
        edif = sb("edif", [P, 2])
        den = sb("den", [P, 2])
        hot = sb("hot", [P, 2, 2, E])
        chosen = sb("chosen", [P, 2, 2, E], BF16)
        both = sb("both", [P, E], BF16)
        sums = sb("sums", [P, 2, E], BF16)
        posf = sb("posf", [P, 2, E])
        prod = sb("prod", [P, 2, 2 * E])
        posk = sb("posk", [P, 2, 2])
        posi = sb("posi", [P, 2, 2, 2], I32)
        tokf = sb("tokf", [P, 2])
        pad = sb("pad", [P, 2, RW])
        o = hi[:, 0, :].bitcast(F32).rearrange("p (b d) -> p b d", b=2)
        rT = hi[:, 1, :].bitcast(F32)
        oT = lo[:, 0, 0:2 * P].bitcast(F32)
        cen = lo[:, 1, :].bitcast(F32).rearrange("p (b d) -> p b d", b=2)
        stackf = pr[:, 0].rearrange("p (a g) m -> p a g m", a=2)
        stackkf = pr[:, 1].rearrange("p (a g) m -> p a g m", a=2)
        hid = prT[:].rearrange("p a (b c d) k -> p (a b) c (d k)", b=2, c=2)
        after_q = qc[:].rearrange("p g t -> p (g t)")
        xt = after_q[:, 0:16 * RW].bitcast(F32).rearrange("p (n h c) -> p n h c", n=4, h=2)
        xth = after_q[:, 4096:4096 + 2 * TW].rearrange("p (n t) -> p n t", n=2)
        xtl = after_q[:, 5120:5120 + 2 * TW].rearrange("p (n t) -> p n t", n=2)
        yw = after_q[:, 6144:6144 + 4 * TW].bitcast(F32).rearrange("p (n h d) -> p n h d", n=2, h=2)
        sg = after_q[:, 8192:8192 + 2048].bitcast(F32).rearrange("p (n c) -> p n c", n=2)
        tb = after_q[:, 10240:10240 + 4096].bitcast(F32)
        ge = tb[:, 0:NT * E].rearrange("p (j e) -> p j e", e=E)
        gw = tb[:, 512:512 + NT * E].rearrange("p (j e) -> p j e", e=E)
        tot = tb[:, 1024:1032]
        toti = tb[:, 1032:1040].bitcast(I32)
        tiles = tb[:, 1040:1048]
        ends = tb[:, 1048:1056]
        step = tb[:, 1056:1064]
        tri = tb[:, 1064:1128].rearrange("p (e f) -> p e f", e=E)
        eidf = tb[:, 1128:1128 + NT]
        srcf = tb[:, 1192:1192 + NT]
        padf = tb[:, 1256:1264]
        eidi = tb[:, 1280:1280 + NT].bitcast(I32)
        srci = tb[:, 1344:1344 + NT].bitcast(I32)
        padi = tb[:, 1408:1416].bitcast(I32)
        yin = kc[:].rearrange("p g t -> p (g t)")[:, 0:16 * GT].bitcast(F32).rearrange(
            "p (n k b d) -> p n k b d", n=4, k=2, b=GB)
        c_iota, c_reg, c_tri, c_row, c_tok = (small[:, SM[n][0]:SM[n][1]] for n in ("iota", "reg", "tri", "row", "tok"))

        S = ctx.enter_context(nc.psum_tensor("S", [P, 4, 512], F32))
        PT = ctx.enter_context(nc.psum_tensor("PT", [P, 2, 512], F32))
        M0 = ctx.enter_context(nc.psum_tensor("M0", [P, 512], F32))
        M1 = ctx.enter_context(nc.psum_tensor("M1", [P, 512], F32))
        RANK, LOGI = 400, 432

        slots = nc.dram_tensor("slots", [DUMP + TW, RW], F32, kind="Internal").ap()
        ys = nc.dram_tensor("ys", [2 * T + TW, P], F32, kind="Internal").ap()

        (s_w, s_c, s_x, s_set, s_setp, s_setq, s_wraw, s_wd, s_wsc, s_wconv) = [sem(n) for n in (
            "weights_in", "consts_in", "x_in", "setup_dve", "setup_pe", "setup_pool",
            "ffn_raw_in", "wd_in", "ffn_split_chain", "ffn_split")]
        s_ctx = [sem("ctx_in_0"), sem("ctx_in_1")]
        (s_st, s_rt, s_xn, s_xnT, s_xnTc, s_kv, s_q, s_hi, s_lo, s_v, s_stk, s_stka, s_stkv) = [sem(n) for n in (
            "ln_chain", "root_ready", "xn_ready", "xnT_psum", "xnT_copied", "kv_psum", "q_psum", "hi_ready",
            "lo_ready", "v_ready", "stacked_psum", "stacked_act", "stacked_dve")]
        s_spare_pool, s_spare_dve = sem("spare_pool"), sem("spare_dve")
        s_kx = [sem("kexp_in_0"), sem("kexp_in_1")]
        (s_sc, s_nm, s_mT, s_mTc, s_sh, s_pr, s_pT, s_pTa, s_pTv, s_pv, s_rs, s_no, s_oT, s_oTc, s_pj,
         s_xb, s_x2) = [sem(n) for n in (
            "scores_psum", "negmax_ready", "maxT_psum", "maxT_copied", "shifted", "probs_ready",
            "probsT_psum", "probsT_act", "probsT_dve", "pv_psum", "rsum_ready", "attn_normed", "oT_psum",
            "oT_copied", "proj_psum", "x_plus_bias", "x2_ready")]
        (s_ra, s_seed, s_nw, s_rows, s_tq, s_rTc, s_lg, s_lgc, s_mx, s_top, s_hotc, s_hot, s_ed, s_rw, s_rk, s_rkc,
         s_pp, s_pos, s_padr, s_zero) = [sem(n) for n in (
            "ln2_chain", "seed_ready", "newton_chain", "rows_ready", "xn2T_psum", "xn2T_copied", "logits_psum",
            "logits_copied", "top_values", "top_ready", "choice_chain", "chosen_ready", "top_exp", "weights_chain",
            "rank_psum", "rank_copied", "position_chain", "positions_ready", "pad_tile_ready", "tok_ready")]
        s_scat = [sem("scattered_0"), sem("scattered_1")]
        (s_tt, s_tot, s_tab, s_padw, s_dump) = [sem(n) for n in (
            "totals_psum", "table_chain", "table_ready", "padding_stored", "dump_stored")]
        s_xt = [sem(f"tile_in_{i}") for i in range(4)]
        (s_tT, s_th, s_tl, s_g, s_u, s_sg, s_h, s_y, s_yw, s_out) = [sem(n) for n in (
            "tileT_psum", "tile_high", "tile_low", "gate_psum", "up_psum", "silu_ready", "hidden_ready", "y_psum",
            "y_weighted", "out_stored")]
        s_add = [sem(f"outputs_scattered_{i}") for i in range(4)]

        s_yin = [sem(f"results_in_{i}") for i in range(4)]
        s_fs, s_fin = sem("first_added"), sem("result_ready")
        xf = a["x"].rearrange("b s d -> s b d")
        ysb = ys[0:2 * T, :].rearrange("(k b s) d -> s k b d", s=P, k=2)
        of = out.rearrange("b s d -> s b d")
        block = ctx.enter_context(nc.Block())
        SCORE_SCALE = float(DK) ** -0.5

        @block.sync
        def _(sp):
            for i in range(2):
                sp.dma_start(x[:, 8 * i:8 * i + 8, :], xf[:, 8 * i:8 * i + 8, :]).then_inc(s_x, 16)
            for t, n in ((wq, "wqT"), (wk, "wkT"), (wv, "wvT"), (wo, "woT"), (bias, "bias"), (gate, "gateT")):
                sp.dma_start(t[:], a[n]).then_inc(s_w, 16)
            for t, n in ((identf, "ident"), (maskf, "mask"), (upperf, "upper"), (small, "small")):
                sp.dma_start(t[:], a[n]).then_inc(s_c, 16)
            sp.dma_start(stackf.rearrange("p a g m -> p (a g m)"), a["stackq"]).then_inc(s_c, 16)
            sp.dma_start(stackkf.rearrange("p a g m -> p (a g m)"), a["stackk"]).then_inc(s_c, 16)
            for i in range(2):
                sp.dma_start(ctxT[:, i, :], a["ctxT"][:, i * GT:(i + 1) * GT]).then_inc(s_ctx[i], 16)
            for i in range(2, 4):
                sp.dma_start(x[:, 8 * i:8 * i + 8, :], xf[:, 8 * i:8 * i + 8, :]).then_inc(s_x, 16)
            with sp.Fori(1, NG // 2) as h:
                for k in range(2):
                    sp.wait_ge(s_kv, h * 2 + (k - 1))
                    sp.dma_start(ctxT[:, k, :], a["ctxT"][:, bass.ds(h * (2 * GT) + k * GT, GT)]).then_inc(s_ctx[k], 16)
            sp.dma_start(wd[:].rearrange("p e c d -> p (e c d)"), a["wdT"]).then_inc(s_wd, 16)
            sp.wait_ge(s_padr, 1)
            sp.dma_start(slots[DUMP:DUMP + TW, :].rearrange("(h p) c -> p h c", p=P), pad[:]).then_inc(s_dump, 16)
            sp.wait_ge(s_setq, 4)
            sp.wait_ge(s_stka, 4 * NG)
            sp.wait_ge(s_stkv, 4 * NG)

            def expand(b, par):
                for s in range(4):
                    sp.dma_start(kexp[32 * s:32 * s + 32, par, :, s, :],
                                 kc[32 * s:32 * s + 32, :, bass.ds(b * P, P)]).then_inc(s_kx[par], 16)

            def pair(h, n):
                if on(n, 0, NPAIR - 1):
                    sp.wait_ge(s_sc, h * 4 + 2)
                    expand(h * 2 + 2, 0)
                if on(n, 0, NPAIR - 1):
                    sp.wait_ge(s_sc, h * 4 + 4)
                    expand(h * 2 + 3, 1)

            expand(0, 0)
            expand(1, 1)
            with sp.Fori(0, NPAIR - 1) as h:
                pair(h, None)
            sp.wait_ge(s_tab, 1)
            for e in range(E):
                r = sp.value_load(padi[0:1, e:e + 1], min_val=0, max_val=DUMP - TW)
                sp.dma_start(slots[bass.ds(r, TW), :].rearrange("(h p) c -> p h c", p=P), pad[:]).then_inc(s_padw, 16)
            sp.wait_ge(s_padw, 16 * E)
            sp.wait_ge(s_dump, 16)
            for r in range(2):
                sp.wait_ge(s_scat[r], 64 * NPAIR // 2)

            def tile_in(j, ring):
                r = sp.value_load(srci[0:1, bass.ds(j, 1)], min_val=0, max_val=DUMP)
                sp.dma_start(xt[:, ring], slots[bass.ds(r, TW), :].rearrange("(h p) c -> p h c", p=P)).then_inc(s_xt[ring], 16)

            for j in range(4):
                tile_in(j, j)
            with sp.Fori(1, NT // 4) as h:
                for r in range(4):
                    sp.wait_ge(s_add[r], h * 32)
                    tile_in(h * 4 + r, r)
            for j in range(NT // 4 * 4, NT):
                sp.wait_ge(s_add[j % 4], 32 * (j // 4))
                tile_in(j, j % 4)
            for r in range(4):
                sp.wait_ge(s_add[r], 32 * ((NT - r + 3) // 4))
            def results_in(i, ring):
                for k in range(2):
                    sp.dma_start(yin[:, ring, k], ysb[:, k, i * GB:i * GB + GB, :]).then_inc(s_yin[ring], 16)

            def results_out(i):
                sp.wait_ge(s_fin, i + 1)
                sp.dma_start(of[:, i * GB:i * GB + GB, :], x[:, i * GB:i * GB + GB, :]).then_inc(s_out, 16)

            for r in range(4):
                results_in(r, r)
            for r in range(4):
                results_out(r)
                results_in(4 + r, r)
            for r in range(4, NG):
                results_out(r)
            sp.wait_ge(s_out, 16 * NG)

        @block.gpsimd
        def _(pool):
            pool.memset(negmT[:], 0.0).then_inc(s_setq, 1)
            pool.memset(eps[:], EPS)
            pool.memset(ones[:], 1.0).then_inc(s_setq, 1)
            pool.memset(v1[:], 1.0).then_inc(s_setq, 1)
            pool.memset(kexp[:], 0.0).then_inc(s_setq, 1)
            pool.memset(sums[:], 0.0)
            pool.memset(rows[:], 0.0)
            pool.memset(pad[:], 0.0).then_inc(s_zero, 1)
            pool.wait_ge(s_c, 96)
            pool.tensor_copy(tokf[:], c_tok).then_inc(s_zero, 1)
            pool.wait_ge(s_zero, 2)
            for h in range(2):
                ins = pool.tensor_scalar(pad[:, h, P:P + 1].bitcast(I32), tokf[:, h:h + 1], 2.0 * T, None, ALU.add)
            ins.then_inc(s_padr, 1)

            for w in range(8):
                hi_w, lo_w = (t[:, 2 * (w % 4):2 * (w % 4) + 2, :] for t in ((wgh, wgl) if w < 4 else (wuh, wul)))
                raw = a["wgT" if w < 4 else "wuT"]
                if w:
                    pool.wait_ge(s_wsc, 3 * w)
                pool.dma_start(stage[:], raw[:, (w % 4) * 1024:(w % 4) * 1024 + 1024]).then_inc(s_wraw, 16)
                pool.wait_ge(s_wraw, 16 * (w + 1))
                st = stage[:].rearrange("p (e f) -> p e f", e=2)
                pool.tensor_scalar(st, st, WSCALE, None, ALU.mult).then_inc(s_wsc, 1)
                pool.wait_ge(s_wsc, 3 * w + 1)
                pool.tensor_copy(hi_w, st).then_inc(s_wsc, 1)
                pool.wait_ge(s_wsc, 3 * w + 2)
                pool.tensor_tensor(lo_w, st, hi_w, ALU.subtract).then_inc(s_wsc, 1)

            def pair(h, par, n):
                if on(n, 2, NPAIR + 2):
                    q = h - 2
                    pool.wait_ge(s_seed, q + 1)
                    c = q * 15
                    src = seed[:]
                    for k in range(3):
                        pool.tensor_tensor(t2[:], src, src, ALU.mult).then_inc(s_nw, 1)
                        pool.wait_ge(s_nw, c + (4 * k + 1))
                        pool.tensor_tensor(t2[:], t2[:], var2[:], ALU.mult).then_inc(s_nw, 1)
                        settle(pool, s_nw, c + (4 * k + 2), s_spare_pool)
                        pool.tensor_scalar(t2[:], t2[:], -0.5, 1.5, ALU.mult, ALU.add).then_inc(s_nw, 1)
                        pool.wait_ge(s_nw, c + (4 * k + 3))
                        pool.tensor_tensor(y2[:], src, t2[:], ALU.mult).then_inc(s_nw, 1)
                        pool.wait_ge(s_nw, c + (4 * k + 4))
                        src = y2[:]
                if on(n, 3, NPAIR + 3):
                    q = h - 3
                    pool.wait_ge(s_top, q + 1)
                    pool.tensor_tensor(chosen[:, 1 - par], hot[:, 0], hot[:, 1], ALU.add).then_inc(s_hotc, 1)
                    pool.wait_ge(s_hotc, q * 2 + 1)
                    pool.tensor_tensor(both[:], chosen[:, 1 - par, 0, :], chosen[:, 1 - par, 1, :], ALU.add).then_inc(s_hotc, 1)
                    pool.wait_ge(s_hotc, q * 2 + 2)
                    pool.tensor_tensor(sums[:, par], sums[:, 1 - par], both[:], ALU.add).then_inc(s_hot, 1)
                if on(n, 2, NPAIR + 2):
                    q = h - 2
                    c = q * 15
                    if n is None:
                        pool.wait_ge(s_scat[par], (h - (4 + par)) * 32 + 64)
                    else:
                        after(pool, s_scat[par], 64 * ((n - 4) // 2 + 1))
                    pool.tensor_tensor(cen, x[:, bass.ds(q * 2, 2), :], mv2[:, :, 0:1].to_broadcast([P, 2, P]),
                                       ALU.subtract).then_inc(s_nw, 1)
                    pool.wait_ge(s_nw, c + 13)
                    pool.tensor_tensor(rows[:, par, :, 0, 0:P], cen, y2[:].unsqueeze(2).to_broadcast([P, 2, P]),
                                       ALU.mult).then_inc(s_nw, 1)
                    settle(pool, s_nw, c + 14, s_spare_pool)
                    pool.tensor_copy(rows[:, par, :, 1, 0:P], rows[:, par, :, 0, 0:P])
                    for k in range(2):
                        ins = pool.tensor_scalar(rows[:, par, :, k, P:P + 1].rearrange("p b c -> p (b c)").bitcast(I32),
                                                 tokf[:], float(k * T), None, ALU.add)
                    ins.then_inc(s_nw, 1)
                    settle(pool, s_nw, c + 15, s_spare_pool)
                    pool.tensor_scalar(tokf[:], tokf[:], 2.0 * P, None, ALU.add).then_inc(s_rows, 1)
                if on(n, 3, NPAIR + 3):
                    settle(pool, s_pos, h - 2, s_spare_pool)
                    for k in range(2):
                        for j in range(2):
                            pool.indirect_dma_start(
                                out=slots[:, :], out_offset=bass.IndirectOffsetOnAxis(ap=posi[:, 1 - par, k, j:j + 1], axis=0),
                                in_=rows[:, 1 - par, j, k, :], in_offset=None).then_inc(s_scat[1 - par], 16)

            for n in range(4):
                pair(n, n % 2, n)
            with pool.Fori(2, (NPAIR - 2) // 2) as hh:
                pair(hh * 2, 0, None)
                pair(hh * 2 + 1, 1, None)
            for n in range(NPAIR - 2, NPAIR + 3):
                pair(n, n % 2, n)

            def add(j, ring, par, before):
                pool.wait_ge(s_yw, j + 1)
                if not (isinstance(before, int) and before == 0):
                    settle(pool, s_add[(ring + 3) % 4], before, s_spare_pool)
                for h in range(2):
                    pool.indirect_dma_start(
                        out=ys[:, :],
                        out_offset=bass.IndirectOffsetOnAxis(ap=xt[:, ring, h, P:P + 1].bitcast(I32), axis=0),
                        in_=yw[:, par, h, :], in_offset=None).then_inc(s_add[ring], 16)

            for j in range(4):
                add(j, j, j % 2, 32 if j else 0)
            with pool.Fori(1, NT // 4) as h:
                for r in range(4):
                    add(h * 4 + r, r, r % 2, h * 32 + (32 if r else 0))
            for j in range(NT // 4 * 4, NT):
                add(j, j % 4, j % 2, 32 * ((j - 1) // 4 + 1))
            for r in range(4):
                pool.wait_ge(s_add[r], 32 * ((NT - r + 3) // 4))

        @block.tensor
        def _(pe):
            pe.wait_ge(s_w, 96)
            pe.wait_ge(s_set, 1)
            pe.matmul(M0[:, 0:P], bob[:], wo[:], start=True, stop=True).then_inc(s_setp, 1)
            pe.wait_ge(s_c, 96)
            pe.wait_ge(s_set, 2)
            pe.wait_ge(s_setq, 2)
            pe.matmul(M0[:, 0:P], ones[:], maskf[:], start=True, stop=True).then_inc(s_setp, 1)
            pe.wait_ge(s_set, 3)

            def project(i, h, k):
                pe.wait_ge(s_ctx[k], h * 16 + 16)
                after(pe, s_lo, i * 2)
                pe.matmul(M0[:], wk[:], ctxT[:, k, :], start=True, stop=True)
                after(pe, s_v, i)
                for j in range(GB):
                    mm = pe.matmul(M1[:, j * P:j * P + P], ctxT[:, k, j * P:j * P + P], wv[:],
                                   start=True, stop=True)
                mm.then_inc(s_kv, 1)
                pe.wait_ge(s_xn, i + 1)
                after(pe, s_xnTc, i)
                for j in range(GB):
                    mm = pe.transpose(PT[:, 0, j * P:j * P + P], xn[:, j, :], identf[:])
                mm.then_inc(s_xnT, 1)
                pe.wait_ge(s_xnTc, i + 1)
                pe.matmul(PT[:, 1, :], wq[:], xnT[:], start=True, stop=True).then_inc(s_q, 1)
                for w, st in ((0, stackk), (1, stackq)):
                    pe.wait_ge(s_lo, i * 2 + w + 1)
                    for g in range(HG):
                        drained = s_stka if g % 2 == 0 else s_stkv
                        after(pe, drained, i * 4 if w == 0 else i * 4 + g // 2 + 1)
                        pe.matmul(S[:, g, :], st[:, 0, g, :], hi[:, w, :], start=True, stop=False)
                        pe.matmul(S[:, g, :], st[:, 1, g, :], lo[:, w, :], start=False, stop=True).then_inc(s_stk, 1)

            project(0, 0, 0)
            project(1, 0, 1)
            with pe.Fori(1, NG // 2) as h:
                project(h * 2, h, 0)
                project(h * 2 + 1, h, 1)
            pe.wait_ge(s_stka, 4 * NG)
            pe.wait_ge(s_stkv, 4 * NG)
            pe.wait_ge(s_v, NG)
            pe.wait_ge(s_lo, 2 * NG)

            def scores(h, s):
                b, g, u = h * 2 + s // 2, s % 2, h * 4 + s
                if g == 0:
                    pe.wait_ge(s_kx[s // 2 % 2], h * 64 + 64 if s < 4 else h * 64 + 128)
                after(pe, s_pr, u - 1)
                for k in range(2):
                    hg = 2 * g + k
                    bank = S[:, 2 * g + k, :]
                    pe.matmul(bank, identb[:], mask4[:].rearrange("p h k -> p (h k)"), start=True, stop=False)
                    mm = pe.matmul(bank, qc[:, hg, bass.ds(b * P, P)],
                                   kexp[:, s // 2 % 2, hg, :, :].rearrange("p s k -> p (s k)"), start=False, stop=True)
                mm.then_inc(s_sc, 1)

            def logits(h):
                pe.wait_ge(s_rTc, h - 2)
                for j in range(2):
                    mm = pe.matmul(M1[:, LOGI + j * E:LOGI + j * E + E], rT[:, j * P:j * P + P], gate[:],
                                   start=True, stop=True)
                mm.then_inc(s_lg, 1)

            def rank(h, ring):
                pe.wait_ge(s_hot, h - 2)
                for j in range(2):
                    dst = M1[:, RANK + j * E:RANK + j * E + E]
                    pe.matmul(dst, onesb[:], sums[:, ring], start=True, stop=False)
                    if j:
                        pe.matmul(dst, onesb[:], chosen[:, ring, 0, :], start=False, stop=False)
                    mm = pe.matmul(dst, upperb[:], chosen[:, ring, j, :], start=False, stop=True)
                mm.then_inc(s_rk, 1)

            def turn_maxima(g, u):
                pe.wait_ge(s_nm, u + 1)
                pe.transpose(M1[0:HU, 256:256 + P], negm[:, g, :], identf[:]).then_inc(s_mT, 1)

            def shift(g, u):
                pe.wait_ge(s_mTc, u + 1)
                for k in range(2):
                    mm = pe.matmul(S[:, 2 * g + k, :], negmT[:],
                                   sel8[:, 4 * k:4 * k + 4, :].rearrange("p h k -> p (h k)"),
                                   start=False, stop=True, skip_group_check=True)
                mm.then_inc(s_sh, 1)

            def turn(g, u):
                pe.wait_ge(s_pr, u + 1)
                for k in range(2):
                    after(pe, s_pTa if k == 0 else s_pTv, u)
                    for hd in range(4):
                        mm = pe.transpose(PT[:, k, hd * P:hd * P + P], pr[:, g, 4 * k + hd, :], identf[:])
                    mm.then_inc(s_pT, 1)

            def pv(b, g, u):
                pe.wait_ge(s_pTa, u + 1)
                pe.wait_ge(s_pTv, u + 1)
                for hd in range(HU):
                    mm = pe.matmul(M1[:, hd * (DK + 1):(hd + 1) * (DK + 1)], prT[:, g, hd, :],
                                   v1[:, bass.ds(b, 1), HU * g + hd, :].rearrange("p a d -> p (a d)"),
                                   start=True, stop=True)
                mm.then_inc(s_pv, 1)

            def pair(h, n, par):
                for s in range(4):
                    g, u = s % 2, h * 4 + s
                    nu = None if n is None else 4 * n + s
                    if on(nu, 0, 4 * NPAIR - 1):
                        scores(h, s + 1)
                    after(pe, s_no, u - 2 if n is None else min(4 * n + s - 2, 2 * NB))
                    if on(nu, 0, 4 * NPAIR):
                        turn_maxima(g, u)
                    if s == 1 and on(n, 3, NPAIR + 3):
                        logits(h)
                    if s == 3 and on(n, 3, NPAIR + 3):
                        rank(h, 1 - par)
                    if on(nu, 0, 4 * NPAIR):
                        shift(g, u)
                    if on(n, 3, NPAIR + 3) and g == 1:
                        pe.wait_ge(s_lgc if s == 1 else s_rkc, h - 2)
                    if on(nu, 1, 4 * NPAIR + 1):
                        turn(1 - g, u - 1)
                    if on(nu, 2, 4 * NPAIR + 2):
                        pv(h * 2 + s // 2 - 1, g, u - 2)
                    b = h * 2 + (s // 2 - 2)
                    nb = None if n is None else 2 * n + s // 2 - 2
                    if g == 0 and on(nb, 0, NB):
                        pe.wait_ge(s_no, b * 2 + 2)
                        after(pe, s_x2, b)
                        if s == 0 and on(n, 3, NPAIR + 3):
                            pe.wait_ge(s_rTc, h - 2)
                        pe.transpose(M0[:, 0:P], o[:, s // 2 % 2, :], identf[:]).then_inc(s_oT, 1)
                    if g == 1 and on(nb, 0, NB):
                        pe.wait_ge(s_oTc, b + 1)
                        if s == 1:
                            pe.matmul(M0[:, P:2 * P], oT, wo[:], start=True, stop=True).then_inc(s_pj, 1)
                    if s == 3 and on(n, 2, NPAIR + 2):
                        pe.wait_ge(s_rows, h - 1)
                        after(pe, s_rTc, h - 2)
                        pe.wait_ge(s_x2, h * 2 - 1 if n is None else min(2 * n - 1, NB))
                        for j in range(2):
                            mm = pe.transpose(M0[:, (2 + j) * P:(3 + j) * P], rows[:, par, j, 0, 0:P], identf[:])
                        mm.then_inc(s_tq, 1)
                    if s == 3 and on(nb, 0, NB):
                        pe.matmul(M0[:, P:2 * P], oT, wo[:], start=True, stop=True).then_inc(s_pj, 1)

            scores(0, 0)
            for n in range(4):
                pair(n, n, n % 2)
            with pe.Fori(2, (NPAIR - 2) // 2) as hh:
                pair(hh * 2, None, 0)
                pair(hh * 2 + 1, None, 1)
            for n in range(NPAIR - 2, NPAIR + 3):
                pair(n, n, n % 2)
            pe.wait_ge(s_rkc, NPAIR)
            pe.wait_ge(s_hot, NPAIR)
            pe.matmul(M1[:, 0:E], onesb[:], sums[:, NPAIR % 2], start=True, stop=True).then_inc(s_tt, 1)

            pe.wait_ge(s_wsc, 24)
            pe.wait_ge(s_wd, 16)
            pe.wait_ge(s_tab, 1)

            def turn_tile(j, ring, par, count):
                pe.wait_ge(s_xt[ring], count)
                after(pe, s_th, j - 1)
                after(pe, s_tl, j - 1)
                bank = M0 if par == 0 else M1
                for k in range(2):
                    mm = pe.transpose(bank[:, k * P:k * P + P], xt[:, ring, k, 0:P], identf[:])
                mm.then_inc(s_tT, 1)

            def gate_up(j, e, hf, par):
                n = j * 2 + hf
                for (ps, wh, wl, free, done) in ((S[:, hf, :], wgh, wgl, s_sg, s_g), (S[:, 2 + hf, :], wuh, wul, s_h, s_u)):
                    after(pe, free, n - 1)
                    for c in range(2):
                        col = (2 * hf + c) * P
                        dst = ps[:, c * TW:c * TW + TW]
                        w_h = wh[:, bass.ds(e, 1), col:col + P].rearrange("p a m -> p (a m)")
                        w_l = wl[:, bass.ds(e, 1), col:col + P].rearrange("p a m -> p (a m)")
                        pe.matmul(dst, w_h, xth[:, par], start=True, stop=False)
                        pe.matmul(dst, w_h, xtl[:, par], start=False, stop=False)
                        mm = pe.matmul(dst, w_l, xth[:, par], start=False, stop=True)
                    mm.then_inc(done, 1)

            def down(j, par):
                e = pe.value_load(eidi[0:1, bass.ds(j, 1)], min_val=0, max_val=E - 1)
                pe.wait_ge(s_h, j * 2 + 2)
                after(pe, s_yw, j - 1)
                for th in range(2):
                    for c in range(FC):
                        mm = pe.matmul(PT[:, par, th * P:th * P + P],
                                       hid[:, 2 * par + c // 2, c % 2, th * P:th * P + P],
                                       wd[:, bass.ds(e, 1), c, :].rearrange("p a d -> p (a d)"),
                                       start=(c == 0), stop=(c == FC - 1))
                mm.then_inc(s_y, 1)

            def tile(j, r, c1, last=False, first=False):
                par = r % 2
                e = pe.value_load(eidi[0:1, bass.ds(j, 1)], min_val=0, max_val=E - 1)
                pe.wait_ge(s_th, j + 1)
                pe.wait_ge(s_tl, j + 1)
                gate_up(j, e, 0, par)
                if not last:
                    turn_tile(j + 1, (r + 1) % 4, 1 - par, c1)
                gate_up(j, e, 1, par)
                if not first:
                    down(j - 1, 1 - par)

            turn_tile(0, 0, 0, 16)
            for j in range(4):
                tile(j, j, 16 if j < 3 else 32, first=j == 0)
            with pe.Fori(1, NT // 4) as h:
                for r in range(4):
                    tile(h * 4 + r, r, h * 16 + (16 if r < 3 else 32))
            for j in range(NT // 4 * 4, NT):
                tile(j, j % 4, 16 * ((j + 1) // 4 + 1), last=j == NT - 1)
            down(NT - 1, (NT - 1) % 2)

        @block.scalar
        def _(act):
            act.wait_ge(s_set, 3)
            act.wait_ge(s_st, NG + 2)
            act.activation(sd[:], mv[:, :, 1], ACT.Sqrt, bias=eps[:, 0:1]).then_inc(s_rt, 1)
            act.wait_ge(s_setq, 3)
            with act.Fori(0, NG) as i:
                act.wait_ge(s_kv, i + 1)
                act.activation(hi[:, 0, :], M0[:], ACT.Identity, bias=bias[:, 1:2]).then_inc(s_hi, 1)
                act.activation(v1[:, bass.ds(i * GB, GB), :, 0:DK],
                               M1[:].rearrange("p (b h d) -> p b h d", b=GB, h=H), ACT.Identity).then_inc(s_v, 1)
                act.wait_ge(s_xnT, i + 1)
                act.activation(xnT[:], PT[:, 0, :], ACT.Identity).then_inc(s_xnTc, 1)
                act.wait_ge(s_q, i + 1)
                act.activation(hi[:, 1, :], PT[:, 1, :], ACT.Identity, bias=bqs[:, 0:1]).then_inc(s_hi, 1)
                for w, dst in ((0, kc), (1, qc)):
                    for g in (0, 2):
                        act.wait_ge(s_stk, i * 8 + 4 * w + g + 1)
                        act.activation(dst[:, g, bass.ds(i * GT, GT)], S[:, g, :], ACT.Identity).then_inc(s_stka, 1)

            def pair(h, n):
                if on(n, 3, NPAIR + 3):
                    act.wait_ge(s_tq, h - 2)
                    act.wait_ge(s_x2, h * 2 - 2 if n is None else min(2 * n - 2, NB))
                    act.activation(rT, M0[:, 2 * P:4 * P], ACT.Identity).then_inc(s_rTc, 1)
                for s in range(4):
                    g, u = s % 2, h * 4 + s
                    nu = None if n is None else 4 * n + s
                    if on(nu, 0, 4 * NPAIR):
                        act.wait_ge(s_sh, u + 1)
                        after(act, s_pT, u * 2 - 2)
                        act.activation(pr[:, g, :, :].rearrange("p (k h) c -> p k (h c)", k=2), S[:, 2 * g:2 * g + 2, :],
                                       ACT.Exp).then_inc(s_pr, 1)
                    if on(nu, 1, 4 * NPAIR + 1):
                        act.wait_ge(s_pT, u * 2 - 1)
                        after(act, s_pv, u - 2)
                        act.activation(prT[:, 1 - g, 0:4, :].rearrange("p h q -> p (h q)"), PT[:, 0, :],
                                       ACT.Identity).then_inc(s_pTa, 1)
                    nb = None if n is None else 2 * n + s // 2 - 2
                    if g == 0 and on(nb, 0, NB):
                        act.wait_ge(s_oT, h * 2 + (s // 2 - 1))
                        act.activation(oT, M0[:, 0:P], ACT.Identity).then_inc(s_oTc, 1)
                    if s == 2 and on(n, 3, NPAIR + 3):
                        act.wait_ge(s_top, h - 2)
                        act.activation(edif[:], dif[:], ACT.Exp).then_inc(s_ed, 1)

            for n in range(4):
                pair(n, n)
            with act.Fori(4, NPAIR - 1) as h:
                pair(h, None)
            for n in range(NPAIR - 1, NPAIR + 3):
                pair(n, n)

            def tile_high(j, par):
                act.wait_ge(s_tT, j + 1)
                after(act, s_u, j * 2 - 2)
                act.activation(xth[:, par], (M0 if par == 0 else M1)[:, 0:TW], ACT.Identity).then_inc(s_th, 1)

            def silu(j, hf):
                act.wait_ge(s_g, j * 2 + (hf + 1))
                after(act, s_h, j * 2 + (hf - 1))
                act.activation(sg[:, hf, :], S[:, hf, :], ACT.Silu, scale=1.0 / WSCALE).then_inc(s_sg, 1)

            def weigh(j, ring, par, left):
                act.wait_ge(s_y, j + 1)
                after(act, s_add[(ring + 2) % 4], left)
                for h in range(2):
                    ins = act.activation(yw[:, par, h, :], PT[:, par, h * P:h * P + P], ACT.Copy,
                                         scale=xt[:, ring, h, P + 1:P + 2])
                ins.then_inc(s_yw, 1)

            def tile(j, r, left, first=False, last=False):
                silu(j, 0)
                if not last:
                    tile_high(j + 1, 1 - r % 2)
                silu(j, 1)
                if not first:
                    weigh(j - 1, (r - 1) % 4, 1 - r % 2, left)

            tile_high(0, 0)
            for j in range(4):
                tile(j, j, 32 if j == 3 else 0, first=j == 0)
            with act.Fori(1, NT // 4) as h:
                for r in range(4):
                    tile(h * 4 + r, r, h * 32 + (32 if r == 3 else 0))
            for j in range(NT // 4 * 4, NT):
                tile(j, j % 4, 32 * ((j - 3) // 4 + 1), last=j == NT - 1)
            weigh(NT - 1, (NT - 1) % 4, (NT - 1) % 2, 32 * ((NT - 3) // 4 + 1))

        @block.vector
        def _(dve):
            dve.wait_ge(s_w, 96)
            dve.wait_ge(s_c, 96)
            dve.wait_ge(s_setq, 2)
            dve.tensor_scalar(bob[:], ones[:], bias[:, 2:3], None, ALU.mult).then_inc(s_set, 1)
            dve.tensor_copy(identb[:], identf[:])
            dve.tensor_copy(upperb[:], upperf[:])
            dve.tensor_copy(onesb[:], ones[:])
            for h in range(4):
                dve.tensor_copy(mask4[:, h, :], maskf[:])
            dve.tensor_copy(stackq[:], stackf)
            dve.tensor_copy(stackk[:], stackkf)
            for h in range(HU):
                dve.tensor_scalar(sel8[:, h, :], ones[:], identf[:, h:h + 1], None, ALU.mult)
            dve.tensor_scalar(bqs[:], bias[:, 0:1], SCORE_SCALE, None, ALU.mult)
            dve.tensor_scalar(wq[:], wq[:], SCORE_SCALE, None, ALU.mult).then_inc(s_st, 1)
            dve.wait_ge(s_st, 1)
            dve.wait_ge(s_setp, 1)
            dve.tensor_copy(bob[:], M0[:, 0:P])
            dve.tensor_scalar(maskf[:], identf[:], bias[:, 3:4], None, ALU.mult).then_inc(s_set, 1)
            dve.wait_ge(s_setp, 2)
            dve.wait_ge(s_set, 2)
            dve.tensor_tensor(bob[:], M0[:, 0:P], bob[:], ALU.add).then_inc(s_set, 1)

            dve.wait_ge(s_x, 64)
            with dve.Fori(0, NG) as i:
                for j in range(GB):
                    b = i * GB + j
                    ins = dve.bn_stats(stats[:, bass.ds(b, 1), :].rearrange("p a d -> p (a d)"),
                                       x[:, bass.ds(b, 1), :].rearrange("p a d -> p (a d)"))
                ins.then_inc(s_st, 1)
            dve.wait_ge(s_st, 1 + NG)
            for b in range(NB):
                ins = dve.bn_aggr(mv[:, b, :], stats[:, b, :])
            ins.then_inc(s_st, 1)
            c0 = NG + 2
            dve.wait_ge(s_st, c0)
            dve.tensor_scalar(nr[:], mv[:, :, 1], EPS, None, ALU.add).then_inc(s_st, 1)
            dve.wait_ge(s_rt, 1)
            dve.reciprocal(rstd[:], sd[:]).then_inc(s_st, 1)
            dve.wait_ge(s_st, c0 + 2)
            dve.tensor_tensor(nr[:], nr[:], rstd[:], ALU.mult).then_inc(s_st, 1)
            dve.wait_ge(s_st, c0 + 3)
            dve.tensor_tensor(nr[:], nr[:], rstd[:], ALU.mult).then_inc(s_st, 1)
            dve.wait_ge(s_st, c0 + 4)
            dve.tensor_scalar(nr[:], nr[:], -0.5, 1.5, ALU.mult, ALU.add).then_inc(s_st, 1)
            dve.wait_ge(s_st, c0 + 5)
            dve.tensor_tensor(rstd[:], rstd[:], nr[:], ALU.mult).then_inc(s_st, 1)
            dve.wait_ge(s_st, c0 + 6)

            def project(i):
                after(dve, s_xnT, i)
                for j in range(GB):
                    ins = dve.tensor_scalar(xn[:, j, :], x[:, bass.ds(i * GB + j, 1), :].rearrange("p a d -> p (a d)"),
                                            mv[:, bass.ds(i * GB + j, 1), 0], rstd[:, bass.ds(i * GB + j, 1)],
                                            ALU.subtract, ALU.mult)
                ins.then_inc(s_xn, 1)
                dve.wait_ge(s_hi, i * 2 + 1)
                dve.scalar_tensor_tensor(lo[:, 0, :], M0[:], bias[:, 1:2], hi[:, 0, :], ALU.add, ALU.subtract).then_inc(s_lo, 1)
                dve.wait_ge(s_hi, i * 2 + 2)
                dve.scalar_tensor_tensor(lo[:, 1, :], PT[:, 1, :], bqs[:, 0:1], hi[:, 1, :], ALU.add, ALU.subtract).then_inc(s_lo, 1)
                for w, dst in ((0, kc), (1, qc)):
                    for g in (1, 3):
                        dve.wait_ge(s_stk, i * 8 + 4 * w + g + 1)
                        dve.tensor_copy(dst[:, g, bass.ds(i * GT, GT)], S[:, g, :]).then_inc(s_stkv, 1)

            project(0)
            with dve.Fori(1, NG) as i:
                project(i)

            def maxima(g, u):
                dve.wait_ge(s_sc, u + 1)
                dve.tensor_reduce(negm[:, g, :], S[:, 2 * g:2 * g + 2, :].rearrange("p k (h c) -> p (k h) c", h=4),
                                  AX_X, ALU.max, negate=True).then_inc(s_nm, 1)

            def norm(g, b2, u):
                dve.wait_ge(s_pv, u + 1)
                po = M1[:, 0:HU * (DK + 1)].rearrange("p (h d) -> p h d", h=HU)
                dve.reciprocal(rsum[:, g, :], po[:, :, DK]).then_inc(s_rs, 1)
                dve.wait_ge(s_rs, u + 1)
                dve.tensor_tensor(o[:, b2, g * 64:g * 64 + 64].rearrange("p (h d) -> p h d", h=HU), po[:, :, 0:DK],
                                  rsum[:, g, :].unsqueeze(2).to_broadcast([P, HU, DK]), ALU.mult).then_inc(s_no, 1)

            def pair(h, n, par):
                for s in range(4):
                    g, u = s % 2, h * 4 + s
                    nu = None if n is None else 4 * n + s
                    if g == 1 and on(n, 3, NPAIR + 3):
                        dve.wait_ge(s_lg if s == 1 else s_rk, h - 2)
                    if on(nu, 0, 4 * NPAIR):
                        dve.wait_ge(s_mT, u + 1)
                        after(dve, s_sh, u)
                        dve.tensor_copy(negmT[0:HU, :], M1[0:HU, 256:256 + P]).then_inc(s_mTc, 1)
                    if s == 1 and on(n, 3, NPAIR + 3):
                        dve.tensor_copy(lg[:].rearrange("p b e -> p (b e)"), M1[:, LOGI:LOGI + 2 * E]).then_inc(s_lgc, 1)
                    if s == 3 and on(n, 3, NPAIR + 3):
                        dve.tensor_tensor(posf[:], M1[:, RANK:RANK + 2 * E].rearrange("p (b e) -> p b e", b=2),
                                          c_reg.unsqueeze(1).to_broadcast([P, 2, E]), ALU.add).then_inc(s_rkc, 1)
                    if on(nu, 0, 4 * NPAIR - 1):
                        maxima(1 - g, u + 1)
                    if on(nu, 1, 4 * NPAIR + 1):
                        dve.wait_ge(s_pT, u * 2)
                        after(dve, s_pv, u - 2)
                        dve.tensor_copy(prT[:, 1 - g, 4:8, :].rearrange("p h q -> p (h q)"), PT[:, 1, :]).then_inc(s_pTv, 1)
                    if on(nu, 2, 4 * NPAIR + 2):
                        after(dve, s_oT, h * 2 + (s // 2 - 2))
                        norm(g, (s // 2 + 1) % 2, u - 2)
                    b = h * 2 + (s // 2 - 2)
                    nb = None if n is None else 2 * n + s // 2 - 2
                    if g == 1 and on(nb, 0, NB):
                        xb = x[:, bass.ds(b, 1), :].rearrange("p a d -> p (a d)")
                        dve.tensor_tensor(xb, xb, bob[:], ALU.add).then_inc(s_xb, 1)
                        dve.wait_ge(s_xb, b + 1)
                        dve.wait_ge(s_pj, b + 1)
                        dve.tensor_tensor(xb, M0[:, P:2 * P], xb, ALU.add).then_inc(s_x2, 1)
                    if s == 0 and on(n, 2, NPAIR + 2):
                        q = h - 2
                        after(dve, s_rows, q)
                        dve.wait_ge(s_x2, h * 2 - 2)
                        for j in range(2):
                            ins = dve.bn_stats(st2[:, j, :], x[:, bass.ds(q * 2 + j, 1), :].rearrange("p a d -> p (a d)"))
                        ins.then_inc(s_ra, 1)
                        settle(dve, s_ra, q * 4 + 1, s_spare_dve)
                        for j in range(2):
                            ins = dve.bn_aggr(mv2[:, j, :], st2[:, j, :])
                        ins.then_inc(s_ra, 1)
                        dve.wait_ge(s_ra, q * 4 + 2)
                        dve.tensor_scalar(var2[:], mv2[:, :, 1], EPS, None, ALU.add).then_inc(s_ra, 1)
                        dve.wait_ge(s_ra, q * 4 + 3)
                        dve.tensor_scalar(seed[:].bitcast(I32), var2[:].bitcast(I32), 1, None,
                                          ALU.arith_shift_right).then_inc(s_ra, 1)
                        dve.wait_ge(s_ra, q * 4 + 4)
                        dve.tensor_scalar(seed[:].bitcast(I32), seed[:].bitcast(I32), -1.0, float(MAGIC),
                                          ALU.mult, ALU.add).then_inc(s_seed, 1)
                    if s == 1 and on(n, 3, NPAIR + 3):
                        q = h - 3
                        settle(dve, s_lgc, q + 1, s_spare_dve)
                        for j in range(2):
                            ins = dve.max(top[:, j, :], lg[:, j, :])
                        ins.then_inc(s_mx, 1)
                        settle(dve, s_mx, q * 2 + 1, s_spare_dve)
                        for j in range(2):
                            ins = dve.max_index(topi[:, j, :], top[:, j, :], lg[:, j, :])
                        ins.then_inc(s_mx, 1)
                        dve.tensor_tensor(dif[:], top[:, :, 1], top[:, :, 0], ALU.subtract)
                        dve.wait_ge(s_mx, q * 2 + 2)
                        dve.tensor_tensor(hot[:], topi[:, :, 0:2].rearrange("p b k -> p k b").unsqueeze(3).to_broadcast([P, 2, 2, E]),
                                          c_iota.unsqueeze(1).unsqueeze(1).to_broadcast([P, 2, 2, E]), ALU.is_equal).then_inc(s_top, 1)
                    if s == 3 and on(n, 3, NPAIR + 3):
                        q, ring = h - 3, 1 - par
                        dve.wait_ge(s_ed, q + 1)
                        dve.tensor_scalar(den[:], edif[:], 1.0, None, ALU.add).then_inc(s_rw, 1)
                        dve.wait_ge(s_rw, q * 2 + 1)
                        w1 = rows[:, ring, :, 0, P + 1]
                        w2 = rows[:, ring, :, 1, P + 1]
                        dve.reciprocal(w1, den[:]).then_inc(s_rw, 1)
                        dve.wait_ge(s_rkc, q + 1)
                        for k in range(2):
                            ins = dve.tensor_tensor(prod[:, k, :], hot[:, k].rearrange("p b e -> p (b e)"),
                                                    posf[:].rearrange("p b e -> p (b e)"), ALU.mult)
                        ins.then_inc(s_pp, 1)
                        dve.wait_ge(s_rw, q * 2 + 2)
                        dve.tensor_tensor(w2, edif[:], w1, ALU.mult)
                        dve.wait_ge(s_pp, q * 2 + 1)
                        dve.tensor_reduce(posk[:], prod[:].rearrange("p k (b e) -> p k b e", b=2), AX_X, ALU.add).then_inc(s_pp, 1)
                        dve.wait_ge(s_pp, q * 2 + 2)
                        dve.tensor_copy(posi[:, ring], posk[:]).then_inc(s_pos, 1)

            maxima(0, 0)
            for n in range(4):
                pair(n, n, n % 2)
            with dve.Fori(2, (NPAIR - 2) // 2) as hh:
                pair(hh * 2, None, 0)
                pair(hh * 2 + 1, None, 1)
            for n in range(NPAIR - 2, NPAIR + 3):
                pair(n, n, n % 2)

            chain = [0]

            def link(ins):
                chain[0] += 1
                ins.then_inc(s_tot, 1)
                dve.wait_ge(s_tot, chain[0])

            dve.wait_ge(s_tt, 1)
            link(dve.tensor_copy(tot, M1[:, 0:E]))
            link(dve.tensor_scalar(toti, tot, float(TW - 1), None, ALU.add))
            link(dve.tensor_scalar(toti, toti, TW.bit_length() - 1, None, ALU.arith_shift_right))
            link(dve.tensor_copy(tiles, toti))
            link(dve.tensor_tensor(tri, c_tri.rearrange("p (e f) -> p e f", e=E), tiles.unsqueeze(1).to_broadcast([P, E, E]), ALU.mult))
            link(dve.tensor_reduce(ends, tri, AX_X, ALU.add))
            link(dve.tensor_scalar(step, tiles, -float(TW), float(REG), ALU.mult, ALU.add))
            link(dve.tensor_scalar(gw[:, :, 0], c_row, 1.0 / TW, None, ALU.mult))
            link(dve.tensor_tensor(ge, gw[:, :, 0:1].to_broadcast([P, NT, E]), ends.unsqueeze(1).to_broadcast([P, NT, E]), ALU.is_ge))
            link(dve.tensor_tensor(gw, ge, step.unsqueeze(1).to_broadcast([P, NT, E]), ALU.mult))
            link(dve.tensor_reduce(eidf, ge, AX_X, ALU.add))
            link(dve.tensor_reduce(srcf, gw, AX_X, ALU.add))
            link(dve.tensor_scalar(eidi, eidf, float(E - 1), None, ALU.min))
            link(dve.tensor_tensor(srcf, srcf, c_row, ALU.add))
            link(dve.tensor_scalar(srci, srcf, float(DUMP), None, ALU.min))
            dve.tensor_tensor(padi, tot, c_reg, ALU.add).then_inc(s_tab, 1)

            def tile_low(j, par):
                dve.wait_ge(s_th, j + 1)
                dve.tensor_tensor(xtl[:, par], (M0 if par == 0 else M1)[:, 0:TW], xth[:, par], ALU.subtract).then_inc(s_tl, 1)

            def hidden(j, hf, par):
                dve.wait_ge(s_sg, j * 2 + (hf + 1))
                dve.wait_ge(s_u, j * 2 + (hf + 1))
                after(dve, s_y, j - 1)
                dve.scalar_tensor_tensor(hid[:, 2 * par + hf, :, :].rearrange("p c t -> p (c t)"), S[:, 2 + hf, :],
                                         1.0 / WSCALE, sg[:, hf, :], ALU.mult, ALU.mult).then_inc(s_h, 1)

            def tile(j, r, last=False):
                hidden(j, 0, r % 2)
                if not last:
                    tile_low(j + 1, 1 - r % 2)
                hidden(j, 1, r % 2)

            tile_low(0, 0)
            for j in range(4):
                tile(j, j)
            with dve.Fori(1, NT // 4) as h:
                for r in range(4):
                    tile(h * 4 + r, r)
            for j in range(NT // 4 * 4, NT):
                tile(j, j % 4, last=j == NT - 1)

            def finish(i, ring, count):
                dve.wait_ge(s_yin[ring], count)
                xb = x[:, i * GB:i * GB + GB, :]
                dve.tensor_tensor(xb, xb, yin[:, ring, 0], ALU.add).then_inc(s_fs, 1)
                dve.wait_ge(s_fs, i + 1)
                dve.tensor_tensor(xb, xb, yin[:, ring, 1], ALU.add).then_inc(s_fin, 1)

            for i in range(NG):
                finish(i, i % 4, 32 + 32 * (i // 4))

_NAMES = ["x", "ctxT", "wqT", "wkT", "wvT", "woT", "bias", "gateT", "wgT", "wuT", "wdT",
          "ident", "mask", "upper", "small", "stackq", "stackk"]


def kernel(x, ctx_1024, L0_xattn_w_q, L0_xattn_b_q, L0_xattn_w_k, L0_xattn_b_k, L0_xattn_w_v, L0_xattn_b_v,
           L0_xattn_w_o, L0_xattn_b_o, L0_ffn_gate_w, L0_ffn_wg, L0_ffn_wu, L0_ffn_wd):
    import numpy as np
    import concourse.bacc as bacc
    from concourse.bass_utils import run_bass_kernel_spmd

    c = np.ascontiguousarray
    stack = np.zeros((2, P, 2, HG, P), np.float32)
    for h in range(H):
        g, s = h // 4, h % 4
        for d in range(DK):
            for t in range(4):
                stack[0, h * DK + d, t // 2, g, 32 * s + DK * t + d] = 1.0
                stack[1, h * DK + d, t % 2, g, 32 * s + DK * t + d] = 1.0
    r = np.arange(P)
    small = np.concatenate([
        np.broadcast_to(np.arange(E), (P, E)),
        np.broadcast_to(np.arange(E) * REG, (P, E)),
        np.broadcast_to(np.tril(np.ones((E, E))).reshape(-1), (P, E * E)),
        np.broadcast_to(np.arange(NT) * TW, (P, NT)),
        np.stack([r, r + P], 1)], 1).astype(np.float32)
    arrays = {
        "x": c(x),
        "ctxT": c(np.asarray(ctx_1024).reshape(T, P).T),
        "wqT": c(np.asarray(L0_xattn_w_q).T), "wkT": c(np.asarray(L0_xattn_w_k).T),
        "wvT": c(np.asarray(L0_xattn_w_v).T), "woT": c(np.asarray(L0_xattn_w_o).T),
        "bias": c(np.stack([np.asarray(v) for v in (L0_xattn_b_q, L0_xattn_b_k, L0_xattn_b_v, L0_xattn_b_o)], 1)),
        "gateT": c(np.asarray(L0_ffn_gate_w).T),
        "wgT": c(np.asarray(L0_ffn_wg).transpose(2, 0, 1).reshape(P, E * FF)),
        "wuT": c(np.asarray(L0_ffn_wu).transpose(2, 0, 1).reshape(P, E * FF)),
        "wdT": c(np.asarray(L0_ffn_wd).transpose(2, 0, 1).reshape(FC, P, E, P).transpose(1, 2, 0, 3).reshape(P, E * FC * P)),
        "ident": np.eye(P, dtype=np.float32),
        "mask": np.where(r[None, :] <= r[:, None], 0.0, -1e30).astype(np.float32),
        "upper": (r[:, None] < r[None, :]).astype(np.float32),
        "small": c(small),
        "stackq": c(stack[0].reshape(P, -1)), "stackk": c(stack[1].reshape(P, -1)),
    }
    nc = bacc.Bacc("TRN2", target_bir_lowering=False, num_devices=1)
    aps = {n: nc.dram_tensor(f"in_{n}", arrays[n].shape, mybir.dt.from_np(arrays[n].dtype), kind="ExternalInput").ap()
           for n in _NAMES}
    out = nc.dram_tensor("out_0", (NB, P, P), F32, kind="ExternalOutput").ap()
    build(nc, aps, out)
    res = run_bass_kernel_spmd(nc, [{f"in_{n}": arrays[n] for n in _NAMES}], core_ids=[0])
    return res.results[0]["out_0"]
```

```python
import concourse.bass as bass
from concourse import mybir
from contextlib import ExitStack

F32 = mybir.dt.float32
F16 = mybir.dt.float16
BF16 = mybir.dt.bfloat16
I32 = mybir.dt.int32
U32 = mybir.dt.uint32
ALU = mybir.AluOpType
ACT = mybir.ActivationFunctionType
AX_X = mybir.AxisListType.X

P = 128
NB = 32
H = 16
DK = P // H
HG = 4
HU = H // 2
E = 8
FF = 512
FC = FF // P
T = NB * P
GB = 4
NG = NB // GB
GT = GB * P
EPS = 1e-5
WSCALE = 64.0
HSCALE = 4.0
XR = 8
VSCALE = 16.0
PSCALE = 1024.0
VW = 2 * (DK + 1)
TW = 256
NT = 2 * T // TW + E - 1
REG = T + TW
DUMP = E * REG
RW = P + 4
MAGIC = 0x5F3759DF
NPAIR = NB // 2


SM, SMALL = {}, 0
for _n, _w in (("iota", E), ("reg", E), ("tri", E * E), ("row", NT), ("tok", 2)):
    SM[_n] = (SMALL, SMALL + _w)
    SMALL += _w


def settle(eng, semaphore, count, spare):
    eng.wait_ge(semaphore, count)
    if not isinstance(count, int):
        eng.sem_inc(spare, 1)


def after(eng, semaphore, count):
    if not (isinstance(count, int) and count <= 0):
        eng.wait_ge(semaphore, count)


def on(n, low, high):
    return n is None or low <= n < high


def build(nc, a, out):
    with ExitStack() as ctx:
        def sb(name, shape, dt=F32):
            return ctx.enter_context(nc.sbuf_tensor(name, shape, dt))

        def sem(name):
            return ctx.enter_context(nc.semaphore(name))

        x = sb("x", [P, NB, P])
        qc = sb("qc", [P, HG, T], F16)
        kc = sb("kc", [P, HG, T], F16)
        v1 = sb("v1", [P, NB, H, 2 * (DK + 1)], F16)
        kexp = sb("kexp", [P, 2, HG, 4, P], F16)
        wgh = sb("wgh", [P, E, FF], F16)
        wgl = sb("wgl", [P, E, FF], F16)
        wuh = sb("wuh", [P, E, FF], F16)
        wul = sb("wul", [P, E, FF], F16)
        wd = sb("wd", [P, E, FC, P])
        stage = sb("stage", [P, 1024])
        ctxT = sb("ctxT", [P, 2, GT])
        wq = sb("wq", [P, P])
        wk = sb("wk", [P, P])
        wv = sb("wv", [P, P])
        wo = sb("wo", [P, P])
        bias = sb("bias", [P, 4])
        bqs = sb("bqs", [P, 1])
        bob = sb("bob", [P, P])
        gate = sb("gate", [P, E])
        identf = sb("identf", [P, P])
        maskf = sb("maskf", [P, P])
        upperf = sb("upperf", [P, P])
        identb = sb("identb", [P, P], BF16)
        nident = sb("nident", [P, P], F16)
        upperb = sb("upperb", [P, P], BF16)
        onesb = sb("onesb", [P, P], BF16)
        mask4 = sb("mask4", [P, 4, P], BF16)
        sel8 = sb("sel8", [P, HU, P], BF16)
        stackq = sb("stackq", [P, 2, HG, P], F16)
        stackk = sb("stackk", [P, 2, HG, P], F16)
        ones = sb("ones", [P, P])
        small = sb("small", [P, SMALL])
        stats = sb("stats", [P, NB, 6])
        mv = sb("mv", [P, NB, 2])
        rstd = sb("rstd", [P, NB])
        sd = sb("sd", [P, NB])
        nr = sb("nr", [P, NB])
        eps = sb("eps", [P, 1])
        xn = sb("xn", [P, GB, P])
        xnT = sb("xnT", [P, GT])
        hi = sb("hi", [P, 2, GT], F16)
        lo = sb("lo", [P, 2, GT], F16)
        negm = sb("negm", [P, 2, HU])
        negmT = sb("negmT", [P, P], BF16)
        pr = sb("pr", [P, 2, HU, P])
        prT = sb("prT", [P, 2, HU, P])
        rsum = sb("rsum", [P, 2, HU])
        osum = sb("osum", [P, 2, HU, DK])
        rows = sb("rows", [P, 2, 2, 2, RW])
        seed = sb("seed", [P, 2])
        var2 = sb("var2", [P, 2])
        y2 = sb("y2", [P, 2])
        t2 = sb("t2", [P, 2])
        mv2 = sb("mv2", [P, 2, 2])
        st2 = sb("st2", [P, 2, 6])
        lg = sb("lg", [P, 2, E])
        top = sb("top", [P, 2, 8])
        topi = sb("topi", [P, 2, 8], U32)
        dif = sb("dif", [P, 2])
        edif = sb("edif", [P, 2])
        den = sb("den", [P, 2])
        hot = sb("hot", [P, 2, 2, E])
        chosen = sb("chosen", [P, 2, 2, E], BF16)
        both = sb("both", [P, E], BF16)
        sums = sb("sums", [P, 2, E], BF16)
        posf = sb("posf", [P, 2, E])
        prod = sb("prod", [P, 2, 2 * E])
        posk = sb("posk", [P, 2, 2])
        posi = sb("posi", [P, 2, 2, 2], I32)
        tokf = sb("tokf", [P, 2])
        pad = sb("pad", [P, 2, RW])
        vb = xnT[:].bitcast(F16)[:, 0:2 * H * VW].rearrange("p (n h d) -> p n h d", n=2, h=H)
        o = hi[:, 0, :].bitcast(F32).rearrange("p (b d) -> p b d", b=2)
        rT = hi[:, 1, :].bitcast(F32)
        oT = lo[:, 0, 0:2 * P].bitcast(F32)
        cen = lo[:, 1, :].bitcast(F32).rearrange("p (b d) -> p b d", b=2)
        prh = prT[:, 0].rearrange("p h q -> p (h q)").bitcast(F16).rearrange("p (u h q) -> p u h q", u=2, h=HU)
        prl = prT[:, 1].rearrange("p h q -> p (h q)").bitcast(F16).rearrange("p (u h q) -> p u h q", u=2, h=HU)
        hid = prT[:].rearrange("p a (b c d) k -> p (a b) c (d k)", b=2, c=2)
        halves = pr[:].rearrange("p a h k -> p (a h k)").bitcast(F16).rearrange("p (w n c t) -> p w n c t", w=2, n=4, c=2)
        hidh, hidl = halves[:, 0], halves[:, 1]
        after_q = qc[:].rearrange("p g t -> p (g t)")
        xt = after_q[:, 0:4 * XR * RW].bitcast(F32).rearrange("p (n h c) -> p n h c", n=XR, h=2)
        xth = after_q[:, 4608:4608 + 2 * TW].rearrange("p (n t) -> p n t", n=2)
        xtl = after_q[:, 5120:5120 + 2 * TW].rearrange("p (n t) -> p n t", n=2)
        yw = after_q[:, 6144:6144 + 4 * TW].bitcast(F32).rearrange("p (n h d) -> p n h d", n=2, h=2)
        sg = after_q[:, 8192:8192 + 2048].bitcast(F32).rearrange("p (n c) -> p n c", n=2)
        tb = after_q[:, 10240:10240 + 4096].bitcast(F32)
        ge = tb[:, 0:NT * E].rearrange("p (j e) -> p j e", e=E)
        gw = tb[:, 512:512 + NT * E].rearrange("p (j e) -> p j e", e=E)
        tot = tb[:, 1024:1032]
        toti = tb[:, 1032:1040].bitcast(I32)
        tiles = tb[:, 1040:1048]
        ends = tb[:, 1048:1056]
        step = tb[:, 1056:1064]
        tri = tb[:, 1064:1128].rearrange("p (e f) -> p e f", e=E)
        eidf = tb[:, 1128:1128 + NT]
        srcf = tb[:, 1192:1192 + NT]
        eidi = tb[:, 1280:1280 + NT].bitcast(I32)
        srci = tb[:, 1344:1344 + NT].bitcast(I32)
        padi = tb[:, 1408:1416].bitcast(I32)
        yin = kc[:].rearrange("p g t -> p (g t)")[:, 0:16 * GT].bitcast(F32).rearrange(
            "p (n k b d) -> p n k b d", n=4, k=2, b=GB)
        wdh, wdl = (kc[:].rearrange("p g t -> p (g t)")[:, 16 * GT + i * E * FF:16 * GT + (i + 1) * E * FF].rearrange(
            "p (e c d) -> p e c d", e=E, c=FC) for i in range(2))
        c_iota, c_reg, c_tri, c_row, c_tok = (small[:, SM[n][0]:SM[n][1]] for n in ("iota", "reg", "tri", "row", "tok"))

        S = ctx.enter_context(nc.psum_tensor("S", [P, 4, 512], F32))
        PT = ctx.enter_context(nc.psum_tensor("PT", [P, 2, 512], F32))
        M0 = ctx.enter_context(nc.psum_tensor("M0", [P, 512], F32))
        M1 = ctx.enter_context(nc.psum_tensor("M1", [P, 512], F32))
        RANK, LOGI = 400, 432

        slots = nc.dram_tensor("slots", [DUMP + TW, RW], F32, kind="Internal").ap()
        ys = nc.dram_tensor("ys", [2 * T + TW, P], F32, kind="Internal").ap()

        (s_w, s_c, s_set, s_setp, s_setq, s_wraw, s_wd, s_wsc) = [sem(n) for n in (
            "weights_in", "consts_in", "setup_dve", "setup_pe", "setup_pool",
            "ffn_raw_in", "wd_in", "ffn_split_chain")]
        s_x = [sem(f"x_in_{i}") for i in range(4)]
        s_ctx = [sem("ctx_in_0"), sem("ctx_in_1")]
        (s_st, s_var, s_rt, s_xn, s_xnT, s_xnTc, s_kv, s_q, s_hi, s_lo, s_v, s_vl, s_stk, s_stka, s_stkv) = [sem(n) for n in (
            "ln_chain", "variances_ready", "root_ready", "xn_ready", "xnT_psum", "xnT_copied", "kv_psum", "q_psum", "hi_ready",
            "lo_ready", "v_high", "v_low", "stacked_psum", "stacked_act", "stacked_dve")]
        s_spare_pool, s_spare_dve = sem("spare_pool"), sem("spare_dve")
        s_kx = [sem("kexp_in_0"), sem("kexp_in_1")]
        s_vb = [sem("vb_in_0"), sem("vb_in_1")]
        (s_sc, s_nm, s_mT, s_mTc, s_sh, s_pr, s_pT, s_pTa, s_sub, s_pl1, s_pTv, s_pv, s_rs, s_no, s_oT, s_oTc, s_pj,
         s_x2) = [sem(n) for n in (
            "scores_psum", "negmax_ready", "maxT_psum", "maxT_copied", "shifted", "probs_ready",
            "probsT_psum", "probsT_high", "probsT_rest", "probsT_low_act", "probsT_low_dve", "pv_psum", "rsum_ready", "attn_normed", "oT_psum",
            "oT_copied", "proj_psum", "x2_ready")]
        (s_ra, s_seed, s_nw, s_rows, s_tq, s_rTc, s_lg, s_lgc, s_mx, s_top, s_hotc, s_hot, s_ed, s_rw, s_rk, s_rkc,
         s_pp, s_pos, s_padr, s_zero) = [sem(n) for n in (
            "ln2_chain", "seed_ready", "newton_chain", "rows_ready", "xn2T_psum", "xn2T_copied", "logits_psum",
            "logits_copied", "top_values", "top_ready", "choice_chain", "chosen_ready", "top_exp", "weights_chain",
            "rank_psum", "rank_copied", "position_chain", "positions_ready", "pad_tile_ready", "tok_ready")]
        s_scat = [sem("scattered_0"), sem("scattered_1")]
        (s_tt, s_tot, s_tab, s_padw, s_dump) = [sem(n) for n in (
            "totals_psum", "table_chain", "table_ready", "padding_stored", "dump_stored")]
        s_xt = [sem(f"tile_in_{i}") for i in range(XR)]
        (s_wdh, s_wdl, s_tT, s_th, s_tl, s_g, s_u, s_sg, s_h, s_hh, s_hl, s_y, s_yw, s_out) = [sem(n) for n in (
            "wd_high", "wd_low", "tileT_psum", "tile_high", "tile_low", "gate_psum", "up_psum", "silu_ready", "hidden_ready", "hidden_high", "hidden_low", "y_psum",
            "y_weighted", "out_stored")]
        s_add = [sem(f"outputs_scattered_{i}") for i in range(XR)]

        s_yin = [sem(f"results_in_{i}") for i in range(4)]
        s_fs, s_fin = sem("first_added"), sem("result_ready")
        xf = a["x"].rearrange("b s d -> s b d")
        ysb = ys[0:2 * T, :].rearrange("(k b s) d -> s k b d", s=P, k=2)
        of = out.rearrange("b s d -> s b d")
        block = ctx.enter_context(nc.Block())

        def padding(queue, experts):
            queue.wait_ge(s_tab, 1)
            for e in experts:
                r = queue.value_load(padi[0:1, e:e + 1], min_val=0, max_val=DUMP - TW)
                queue.dma_start(slots[bass.ds(r, TW), :].rearrange("(h p) c -> p h c", p=P), pad[:]).then_inc(s_padw, 16)

        SCORE_SCALE = float(DK) ** -0.5

        @block.sync
        def _(sp):
            for i in range(2):
                sp.dma_start(x[:, 8 * i:8 * i + 8, :], xf[:, 8 * i:8 * i + 8, :]).then_inc(s_x[i], 16)
            sp.dma_start(ctxT[:, 0, :], a["ctxT"][:, 0:GT]).then_inc(s_ctx[0], 16)
            for i in range(2, 4):
                sp.dma_start(x[:, 8 * i:8 * i + 8, :], xf[:, 8 * i:8 * i + 8, :]).then_inc(s_x[i], 16)
            sp.dma_start(ctxT[:, 1, :], a["ctxT"][:, GT:2 * GT]).then_inc(s_ctx[1], 16)
            with sp.Fori(1, NG // 2) as h:
                for k in range(2):
                    sp.wait_ge(s_kv, h * 2 + (k - 1))
                    sp.dma_start(ctxT[:, k, :], a["ctxT"][:, bass.ds(h * (2 * GT) + k * GT, GT)]).then_inc(s_ctx[k], 16)
            sp.dma_start(wd[:].rearrange("p e c d -> p (e c d)"), a["wdT"]).then_inc(s_wd, 16)
            sp.wait_ge(s_padr, 1)
            sp.dma_start(slots[DUMP:DUMP + TW, :].rearrange("(h p) c -> p h c", p=P), pad[:]).then_inc(s_dump, 16)
            sp.wait_ge(s_setq, 4)
            sp.wait_ge(s_stka, 4 * NG)
            sp.wait_ge(s_stkv, 4 * NG)
            sp.wait_ge(s_v, NG)
            sp.wait_ge(s_vl, NG)

            def expand(b, par):
                for s in range(4):
                    sp.dma_start(kexp[32 * s:32 * s + 32, par, :, s, :],
                                 kc[32 * s:32 * s + 32, :, bass.ds(b * P, P)]).then_inc(s_kx[par], 16)

            def fetch_v(b, par):
                sp.dma_start(vb[:, par], v1[:, bass.ds(b, 1), :, :].rearrange("p a h d -> p (a h) d")).then_inc(s_vb[par], 16)

            def pair(h, last=False):
                if not last:
                    sp.wait_ge(s_sc, h * 4 + 2)
                    expand(h * 2 + 2, 0)
                after(sp, s_pv, h * 4)
                fetch_v(h * 2 + 1, 1)
                if not last:
                    sp.wait_ge(s_sc, h * 4 + 4)
                    expand(h * 2 + 3, 1)
                    sp.wait_ge(s_pv, h * 4 + 2)
                    fetch_v(h * 2 + 2, 0)

            expand(0, 0)
            expand(1, 1)
            fetch_v(0, 0)
            pair(0)
            with sp.Fori(1, NPAIR - 1) as h:
                pair(h)
            pair(NPAIR - 1, last=True)
            padding(sp, range(0, E // 2))
            sp.wait_ge(s_padw, 16 * E)
            sp.wait_ge(s_dump, 16)
            for r in range(2):
                sp.wait_ge(s_scat[r], 64 * NPAIR // 2)

            def tile_in(j, ring):
                r = sp.value_load(srci[0:1, bass.ds(j, 1)], min_val=0, max_val=DUMP)
                sp.dma_start(xt[:, ring], slots[bass.ds(r, TW), :].rearrange("(h p) c -> p h c", p=P)).then_inc(s_xt[ring], 16)

            for j in range(XR):
                tile_in(j, j)
            with sp.Fori(1, NT // XR) as h:
                for r in range(XR):
                    sp.wait_ge(s_add[r], h * 32)
                    tile_in(h * XR + r, r)
            for j in range(NT // XR * XR, NT):
                sp.wait_ge(s_add[j % XR], 32 * (j // XR))
                tile_in(j, j % XR)
            for r in range(XR):
                sp.wait_ge(s_add[r], 32 * ((NT - r + XR - 1) // XR))
            def results_in(i, ring):
                for k in range(2):
                    sp.dma_start(yin[:, ring, k], ysb[:, k, i * GB:i * GB + GB, :]).then_inc(s_yin[ring], 16)

            def results_out(i):
                sp.wait_ge(s_fin, i + 1)
                sp.dma_start(of[:, i * GB:i * GB + GB, :], x[:, i * GB:i * GB + GB, :]).then_inc(s_out, 16)

            for r in range(4):
                results_in(r, r)
            for r in range(4):
                results_out(r)
                results_in(4 + r, r)
            for r in range(4, NG):
                results_out(r)
            sp.wait_ge(s_out, 16 * NG)

        @block.gpsimd
        def _(pool):
            pool.memset(negmT[:], 0.0).then_inc(s_setq, 1)
            pool.memset(eps[:], EPS)
            pool.memset(ones[:], 1.0).then_inc(s_setq, 1)
            pool.memset(v1[:, :, :, DK:DK + 1], VSCALE)
            pool.memset(v1[:, :, :, 2 * DK + 1:], 0.0).then_inc(s_setq, 1)
            pool.memset(kexp[:], 0.0).then_inc(s_setq, 1)
            pool.memset(sums[:], 0.0)
            pool.memset(rows[:], 0.0)
            pool.memset(pad[:], 0.0).then_inc(s_zero, 1)
            pool.wait_ge(s_c, 80)
            pool.tensor_copy(tokf[:], c_tok).then_inc(s_zero, 1)
            pool.wait_ge(s_zero, 2)
            for h in range(2):
                ins = pool.tensor_scalar(pad[:, h, P:P + 1].bitcast(I32), tokf[:, h:h + 1], 2.0 * T, None, ALU.add)
            ins.then_inc(s_padr, 1)

            for w in range(8):
                hi_w, lo_w = (t[:, 2 * (w % 4):2 * (w % 4) + 2, :] for t in ((wgh, wgl) if w < 4 else (wuh, wul)))
                raw = a["wgT" if w < 4 else "wuT"]
                if w:
                    pool.wait_ge(s_wsc, 3 * w)
                pool.dma_start(stage[:], raw[:, (w % 4) * 1024:(w % 4) * 1024 + 1024]).then_inc(s_wraw, 16)
                pool.wait_ge(s_wraw, 16 * (w + 1))
                st = stage[:].rearrange("p (e f) -> p e f", e=2)
                pool.tensor_scalar(st, st, WSCALE, None, ALU.mult).then_inc(s_wsc, 1)
                pool.wait_ge(s_wsc, 3 * w + 1)
                pool.tensor_copy(hi_w, st).then_inc(s_wsc, 1)
                pool.wait_ge(s_wsc, 3 * w + 2)
                pool.tensor_tensor(lo_w, st, hi_w, ALU.subtract).then_inc(s_wsc, 1)

            NW = 14

            def pair(h, par, n):
                if on(n, 2, NPAIR + 2):
                    q = h - 2
                    pool.wait_ge(s_seed, q + 1)
                    c = q * NW
                    src = seed[:]
                    for k in range(3):
                        pool.tensor_tensor(t2[:], src, src, ALU.mult).then_inc(s_nw, 1)
                        pool.wait_ge(s_nw, c + (4 * k + 1))
                        pool.tensor_tensor(t2[:], t2[:], var2[:], ALU.mult).then_inc(s_nw, 1)
                        settle(pool, s_nw, c + (4 * k + 2), s_spare_pool)
                        pool.tensor_scalar(t2[:], t2[:], -0.5, 1.5, ALU.mult, ALU.add).then_inc(s_nw, 1)
                        pool.wait_ge(s_nw, c + (4 * k + 3))
                        pool.tensor_tensor(y2[:], src, t2[:], ALU.mult).then_inc(s_nw, 1)
                        pool.wait_ge(s_nw, c + (4 * k + 4))
                        src = y2[:]
                if on(n, 3, NPAIR + 3):
                    q = h - 3
                    pool.wait_ge(s_top, q + 1)
                    pool.tensor_tensor(chosen[:, 1 - par], hot[:, 0], hot[:, 1], ALU.add).then_inc(s_hotc, 1)
                    pool.wait_ge(s_hotc, q * 2 + 1)
                    pool.tensor_tensor(both[:], chosen[:, 1 - par, 0, :], chosen[:, 1 - par, 1, :], ALU.add).then_inc(s_hotc, 1)
                    pool.wait_ge(s_hotc, q * 2 + 2)
                    pool.tensor_tensor(sums[:, par], sums[:, 1 - par], both[:], ALU.add).then_inc(s_hot, 1)
                if on(n, 2, NPAIR + 2):
                    q = h - 2
                    c = q * NW
                    if n is None:
                        pool.wait_ge(s_scat[par], (h - (4 + par)) * 32 + 64)
                    else:
                        after(pool, s_scat[par], 64 * ((n - 4) // 2 + 1))
                    pool.tensor_tensor(cen, x[:, bass.ds(q * 2, 2), :], mv2[:, :, 0:1].to_broadcast([P, 2, P]),
                                       ALU.subtract).then_inc(s_nw, 1)
                    pool.wait_ge(s_nw, c + 13)
                    for k in range(2):
                        pool.tensor_tensor(rows[:, par, :, k, 0:P], cen, y2[:].unsqueeze(2).to_broadcast([P, 2, P]), ALU.mult)
                    for k in range(2):
                        ins = pool.tensor_scalar(rows[:, par, :, k, P:P + 1].rearrange("p b c -> p (b c)").bitcast(I32),
                                                 tokf[:], float(k * T), None, ALU.add)
                    ins.then_inc(s_nw, 1)
                    settle(pool, s_nw, c + 14, s_spare_pool)
                    pool.tensor_scalar(tokf[:], tokf[:], 2.0 * P, None, ALU.add).then_inc(s_rows, 1)
                if on(n, 3, NPAIR + 3):
                    settle(pool, s_pos, h - 2, s_spare_pool)
                    for k in range(2):
                        for j in range(2):
                            pool.indirect_dma_start(
                                out=slots[:, :], out_offset=bass.IndirectOffsetOnAxis(ap=posi[:, 1 - par, k, j:j + 1], axis=0),
                                in_=rows[:, 1 - par, j, k, :], in_offset=None).then_inc(s_scat[1 - par], 16)

            for n in range(4):
                pair(n, n % 2, n)
            with pool.Fori(2, (NPAIR - 2) // 2) as hh:
                pair(hh * 2, 0, None)
                pair(hh * 2 + 1, 1, None)
            for n in range(NPAIR - 2, NPAIR + 3):
                pair(n, n % 2, n)

            def add(j, ring, par, before):
                pool.wait_ge(s_yw, j + 1)
                if not (isinstance(before, int) and before == 0):
                    settle(pool, s_add[(ring - 1) % XR], before, s_spare_pool)
                for h in range(2):
                    pool.indirect_dma_start(
                        out=ys[:, :],
                        out_offset=bass.IndirectOffsetOnAxis(ap=xt[:, ring, h, P:P + 1].bitcast(I32), axis=0),
                        in_=yw[:, par, h, :], in_offset=None).then_inc(s_add[ring], 16)

            for j in range(XR):
                add(j, j, j % 2, 32 if j else 0)
            with pool.Fori(1, NT // XR) as h:
                for r in range(XR):
                    add(h * XR + r, r, r % 2, h * 32 + (32 if r else 0))
            for j in range(NT // XR * XR, NT):
                add(j, j % XR, j % 2, 32 * ((j - 1) // XR + 1))
            for r in range(XR):
                pool.wait_ge(s_add[r], 32 * ((NT - r + XR - 1) // XR))

        @block.tensor
        def _(pe):
            pe.wait_ge(s_w, 112)
            pe.wait_ge(s_set, 1)
            pe.matmul(M0[:, 0:P], bob[:], wo[:], start=True, stop=True).then_inc(s_setp, 1)
            pe.wait_ge(s_c, 80)
            pe.wait_ge(s_set, 2)
            pe.wait_ge(s_setq, 2)
            pe.matmul(M0[:, 0:P], ones[:], maskf[:], start=True, stop=True).then_inc(s_setp, 1)
            pe.wait_ge(s_set, 3)

            def keys_values(i, count, k):
                pe.wait_ge(s_ctx[k], count)
                after(pe, s_lo, i * 2 - 1)
                pe.matmul(M0[:], wk[:], ctxT[:, k, :], start=True, stop=True)
                after(pe, s_vl, i)
                for j in range(GB):
                    mm = pe.matmul(M1[:, j * P:j * P + P], ctxT[:, k, j * P:j * P + P], wv[:],
                                   start=True, stop=True)
                mm.then_inc(s_kv, 1)
                pe.wait_ge(s_xn, i + 1)
                after(pe, s_xnTc, i)
                for j in range(GB):
                    mm = pe.transpose(PT[:, 0, j * P:j * P + P], xn[:, j, :], identf[:])
                mm.then_inc(s_xnT, 1)

            def queries(i):
                pe.wait_ge(s_xnTc, i + 1)
                after(pe, s_lo, i * 2)
                pe.matmul(PT[:, 1, :], wq[:], xnT[:], start=True, stop=True).then_inc(s_q, 1)

            def stack(i, w):
                st = stackq if w else stackk
                pe.wait_ge(s_lo, i * 2 + w + 1)
                for g in range(HG):
                    after(pe, s_stka if g % 2 == 0 else s_stkv, i * 4 + (2 * w - 1 + g // 2))
                    pe.matmul(S[:, g, :], st[:, 0, g, :], hi[:, w, :], start=True, stop=False)
                    pe.matmul(S[:, g, :], st[:, 1, g, :], lo[:, w, :], start=False, stop=True).then_inc(s_stk, 1)

            def project(i, count, k):
                stack(i, 0)
                keys_values(i + 1, count, k)
                stack(i, 1)
                queries(i + 1)

            keys_values(0, 16, 0)
            queries(0)
            project(0, 16, 1)
            with pe.Fori(1, NG // 2) as h:
                project(h * 2 - 1, h * 16 + 16, 0)
                project(h * 2, h * 16 + 16, 1)
            stack(NG - 1, 0)
            stack(NG - 1, 1)
            pe.wait_ge(s_stka, 4 * NG)
            pe.wait_ge(s_stkv, 4 * NG)
            pe.wait_ge(s_vl, NG)
            pe.wait_ge(s_lo, 2 * NG)

            def scores(h, s, banks=(0, 1)):
                b, g, u = h * 2 + s // 2, s % 2, h * 4 + s
                if banks[0] == 0:
                    if g == 0:
                        pe.wait_ge(s_kx[s // 2 % 2], h * 64 + 64 if s < 4 else h * 64 + 128)
                    after(pe, s_pr, u - 1)
                for k in banks:
                    hg = 2 * g + k
                    bank = S[:, 2 * g + k, :]
                    pe.matmul(bank, identb[:], mask4[:].rearrange("p h k -> p (h k)"), start=True, stop=False)
                    mm = pe.matmul(bank, qc[:, hg, bass.ds(b * P, P)],
                                   kexp[:, s // 2 % 2, hg, :, :].rearrange("p s k -> p (s k)"), start=False, stop=True)
                if banks[-1] == 1:
                    mm.then_inc(s_sc, 1)

            def logits(h):
                pe.wait_ge(s_rTc, h - 2)
                for j in range(2):
                    mm = pe.matmul(M1[:, LOGI + j * E:LOGI + j * E + E], rT[:, j * P:j * P + P], gate[:],
                                   start=True, stop=True)
                mm.then_inc(s_lg, 1)

            def rank(h, ring):
                pe.wait_ge(s_hot, h - 2)
                for j in range(2):
                    dst = M1[:, RANK + j * E:RANK + j * E + E]
                    pe.matmul(dst, onesb[:], sums[:, ring], start=True, stop=False)
                    if j:
                        pe.matmul(dst, onesb[:], chosen[:, ring, 0, :], start=False, stop=False)
                    mm = pe.matmul(dst, upperb[:], chosen[:, ring, j, :], start=False, stop=True)
                mm.then_inc(s_rk, 1)

            def turn_maxima(g, u):
                pe.wait_ge(s_nm, u + 1)
                pe.transpose(M1[0:HU, 256:256 + P], negm[:, g, :], identf[:]).then_inc(s_mT, 1)

            def shift(g, u):
                pe.wait_ge(s_mTc, u + 1)
                for k in range(2):
                    mm = pe.matmul(S[:, 2 * g + k, :], negmT[:],
                                   sel8[:, 4 * k:4 * k + 4, :].rearrange("p h k -> p (h k)"),
                                   start=False, stop=True, skip_group_check=True)
                mm.then_inc(s_sh, 1)

            def turn(g, u, k):
                pe.wait_ge(s_pr, u + 1)
                after(pe, (s_pTv, s_pl1)[k], u)
                for hd in range(4):
                    mm = pe.matmul(PT[:, k, hd * P:hd * P + P], pr[:, g, 4 * k + hd, :], identf[:],
                                   start=(hd == 0), stop=True, is_transpose=True, skip_group_check=True)
                mm.then_inc(s_pT, 1)

            def rest(g, u):
                pe.wait_ge(s_pTa, u * 2 + 2)
                pe.matmul(PT[:, 1, :], nident[:], prh[:, g, 4:8, :].rearrange("p h q -> p (h q)"),
                          start=False, stop=True, skip_group_check=True).then_inc(s_sub, 1)

            def pv(g, u, par, count):
                if g == 0:
                    pe.wait_ge(s_vb[par], count)
                pe.wait_ge(s_pTv, u + 1)
                pe.wait_ge(s_pl1, u + 1)
                for hd in range(HU):
                    dst = M1[:, hd * VW:(hd + 1) * VW]
                    vh = vb[:, par, HU * g + hd, :]
                    pe.matmul(dst, prh[:, g, hd, :], vh, start=True, stop=False)
                    mm = pe.matmul(dst, prl[:, g, hd, :], vh, start=False, stop=True)
                mm.then_inc(s_pv, 1)

            def pair(h, n, par):
                for s in range(4):
                    g, u = s % 2, h * 4 + s
                    nu = None if n is None else 4 * n + s
                    nb = None if n is None else 2 * n + s // 2 - 2
                    b = h * 2 + (s // 2 - 2)
                    if on(nu, 1, 4 * NPAIR + 1):
                        turn(1 - g, u - 1, 0)
                    after(pe, s_no, u - 3 if n is None else min(4 * n + s - 3, 2 * NB))
                    if on(nu, 0, 4 * NPAIR):
                        turn_maxima(g, u)
                    if s == 1 and on(n, 3, NPAIR + 3):
                        logits(h)
                    if s == 3 and on(n, 3, NPAIR + 3):
                        rank(h, 1 - par)
                    if s == 0 and on(n, 3, NPAIR + 3):
                        pe.wait_ge(s_rows, h - 2)
                        after(pe, s_rTc, h - 3)
                        pe.wait_ge(s_x2, h * 2 - 2 if n is None else min(2 * n - 2, NB))
                        for j in range(2):
                            mm = pe.transpose(M0[:, (2 + j) * P:(3 + j) * P], rows[:, 1 - par, j, 0, 0:P], identf[:])
                        mm.then_inc(s_tq, 1)
                    if on(nu, 1, 4 * NPAIR + 1):
                        turn(1 - g, u - 1, 1)
                    if on(nu, 0, 4 * NPAIR):
                        shift(g, u)
                    if on(nu, 0, 4 * NPAIR - 1):
                        scores(h, s + 1)
                    if on(nu, 1, 4 * NPAIR + 1):
                        rest(1 - g, u - 1)
                    if g == 1 and on(nb, 0, NB):
                        pe.wait_ge(s_oTc, b + 1)
                        pe.matmul(M0[:, P:2 * P], identf[:], bob[:], start=True, stop=False)
                        pe.matmul(M0[:, P:2 * P], oT, wo[:], start=False, stop=True).then_inc(s_pj, 1)
                    if on(n, 3, NPAIR + 3) and g == 1:
                        pe.wait_ge(s_lgc if s == 1 else s_rkc, h - 2)
                    if on(nu, 2, 4 * NPAIR + 2):
                        after(pe, s_no, u - 2)
                        pv(g, u - 2, 1 if s < 2 else 0, h * 16 if s < 2 else h * 16 + 16)
                    if g == 0 and on(nb, 0, NB):
                        pe.wait_ge(s_no, b * 2 + 2)
                        after(pe, s_x2, b)
                        if s == 0 and on(n, 3, NPAIR + 3):
                            pe.wait_ge(s_rTc, h - 2)
                        pe.transpose(M0[:, 0:P], o[:, s // 2 % 2, :], identf[:]).then_inc(s_oT, 1)

            scores(0, 0)
            for n in range(4):
                pair(n, n, n % 2)
            with pe.Fori(2, (NPAIR - 2) // 2) as hh:
                pair(hh * 2, None, 0)
                pair(hh * 2 + 1, None, 1)
            for n in range(NPAIR - 2, NPAIR + 3):
                pair(n, n, n % 2)
            pe.wait_ge(s_rkc, NPAIR)
            pe.wait_ge(s_hot, NPAIR)
            pe.matmul(M1[:, 0:E], onesb[:], sums[:, NPAIR % 2], start=True, stop=True).then_inc(s_tt, 1)

            pe.wait_ge(s_wsc, 24)
            pe.wait_ge(s_tab, 1)
            pe.wait_ge(s_wdl, E)

            def turn_tile(j, ring, par, count):
                pe.wait_ge(s_xt[ring], count)
                after(pe, s_th, j - 1)
                after(pe, s_tl, j - 1)
                bank = M0 if par == 0 else M1
                for k in range(2):
                    mm = pe.transpose(bank[:, k * P:k * P + P], xt[:, ring, k, 0:P], identf[:])
                mm.then_inc(s_tT, 1)

            def gate_up(j, e, hf, par):
                n = j * 2 + hf
                for (ps, wh, wl, free, done) in ((S[:, hf, :], wgh, wgl, s_sg, s_g), (S[:, 2 + hf, :], wuh, wul, s_h, s_u)):
                    after(pe, free, n - 1)
                    for c in range(2):
                        col = (2 * hf + c) * P
                        dst = ps[:, c * TW:c * TW + TW]
                        w_h = wh[:, bass.ds(e, 1), col:col + P].rearrange("p a m -> p (a m)")
                        w_l = wl[:, bass.ds(e, 1), col:col + P].rearrange("p a m -> p (a m)")
                        pe.matmul(dst, w_h, xth[:, par], start=True, stop=False)
                        pe.matmul(dst, w_h, xtl[:, par], start=False, stop=False)
                        mm = pe.matmul(dst, w_l, xth[:, par], start=False, stop=True)
                    mm.then_inc(done, 1)

            def down(j, par, e):
                pe.wait_ge(s_hl, j * 2 + 2)
                after(pe, s_yw, j - 1)
                for c in range(FC):
                    w_h, w_l = (t[:, bass.ds(e, 1), c, :].rearrange("p a d -> p (a d)") for t in (wdh, wdl))
                    for k, (h, w) in enumerate(((hidh, w_h), (hidl, w_h), (hidh, w_l))):
                        for th in range(2):
                            mm = pe.matmul(PT[:, par, th * P:th * P + P], h[:, 2 * par + c // 2, c % 2, th * P:th * P + P], w,
                                           start=(c + k + th == 0), stop=(c == FC - 1 and k == 2), skip_group_check=True)
                mm.then_inc(s_y, 1)

            def expert(j):
                return pe.value_load(eidi[0:1, bass.ds(j, 1)], min_val=0, max_val=E - 1)

            def tile(j, r, c1, e, e_last, more=False):
                par = r % 2
                pe.wait_ge(s_th, j + 1)
                pe.wait_ge(s_tl, j + 1)
                gate_up(j, e, 0, par)
                if c1 is not None:
                    turn_tile(j + 1, (r + 1) % XR, 1 - par, c1)
                e_next = expert(j + 1) if more else None
                gate_up(j, e, 1, par)
                if e_last is not None:
                    down(j - 1, 1 - par, e_last)
                return e_next

            turn_tile(0, 0, 0, 16)
            e, e_last = expert(0), None
            for j in range(XR):
                e, e_last = tile(j, j, 16 if j < XR - 1 else 32, e, e_last, more=j < XR - 1), e
            with pe.Fori(1, NT // XR) as h:
                e, e_last = expert(h * XR), expert(h * XR - 1)
                for r in range(XR):
                    e, e_last = tile(h * XR + r, r, h * 16 + (16 if r < XR - 1 else 32), e, e_last, more=r < XR - 1), e
            e, e_last = expert(NT // XR * XR), expert(NT // XR * XR - 1)
            for j in range(NT // XR * XR, NT):
                e, e_last = tile(j, j % XR, 16 * ((j + 1) // XR + 1) if j < NT - 1 else None, e, e_last, more=j < NT - 1), e
            down(NT - 1, (NT - 1) % 2, e_last)

        @block.scalar
        def _(act):
            for t, n in ((identf, "ident"), (bias, "bias"), (wk, "wkT"), (wv, "wvT"), (wo, "woT"), (wq, "wqT"), (gate, "gateT")):
                act.dma_start(t[:], a[n]).then_inc(s_w, 16)
            for t, n in ((maskf, "mask"), (upperf, "upper"), (small, "small")):
                act.dma_start(t[:], a[n]).then_inc(s_c, 16)
            act.dma_start(stackk[:].rearrange("p a g m -> p (a g m)"), a["stackk"]).then_inc(s_c, 16)
            act.dma_start(stackq[:].rearrange("p a g m -> p (a g m)"), a["stackq"]).then_inc(s_c, 16)

            def root(hf):
                act.wait_ge(s_var, hf + 1)
                act.activation(sd[:, 16 * hf:16 * hf + 16], mv[:, 16 * hf:16 * hf + 16, 1], ACT.Sqrt,
                               bias=eps[:, 0:1]).then_inc(s_rt, 1)

            def keys_values(i):
                act.wait_ge(s_kv, i + 1)
                act.activation(hi[:, 0, :], M0[:], ACT.Identity, bias=bias[:, 1:2]).then_inc(s_hi, 1)
                act.activation(v1[:, bass.ds(i * GB, GB), :, 0:DK],
                               M1[:].rearrange("p (b h d) -> p b h d", b=GB, h=H), ACT.Identity, scale=VSCALE).then_inc(s_v, 1)
                act.wait_ge(s_xnT, i + 1)
                act.activation(xnT[:], PT[:, 0, :], ACT.Identity).then_inc(s_xnTc, 1)

            def queries(i):
                act.wait_ge(s_q, i + 1)
                act.activation(hi[:, 1, :], PT[:, 1, :], ACT.Identity, bias=bqs[:, 0:1]).then_inc(s_hi, 1)

            def stacked(i, w):
                for g in (0, 2):
                    act.wait_ge(s_stk, i * 8 + (4 * w + g + 1))
                    act.activation((qc if w else kc)[:, g, bass.ds(i * GT, GT)], S[:, g, :], ACT.Identity).then_inc(s_stka, 1)

            def project(i):
                stacked(i, 0)
                keys_values(i + 1)
                stacked(i, 1)
                queries(i + 1)

            act.wait_ge(s_setq, 2)
            root(0)
            act.wait_ge(s_set, 3)
            keys_values(0)
            root(1)
            queries(0)
            project(0)
            with act.Fori(1, NG - 1) as i:
                project(i)
            stacked(NG - 1, 0)
            stacked(NG - 1, 1)

            def high(g, u, k):
                act.wait_ge(s_pT, u * 2 + (k + 1))
                act.activation(prh[:, g, 4 * k:4 * k + 4, :].rearrange("p h q -> p (h q)"), PT[:, k, :],
                               ACT.Identity, scale=PSCALE).then_inc(s_pTa, 1)

            def pair(h, n):
                for s in range(4):
                    g, u = s % 2, h * 4 + s
                    nu = None if n is None else 4 * n + s
                    if s == 2 and on(n, 3, NPAIR + 3):
                        act.wait_ge(s_top, h - 2)
                        act.activation(edif[:], dif[:], ACT.Exp).then_inc(s_ed, 1)
                    if on(nu, 1, 4 * NPAIR + 1):
                        after(act, s_pv, u - 2)
                        high(1 - g, u - 1, 0)
                    if s == 0 and on(n, 3, NPAIR + 3):
                        act.wait_ge(s_tq, h - 2)
                        act.activation(rT, M0[:, 2 * P:4 * P], ACT.Identity).then_inc(s_rTc, 1)
                    if on(nu, 1, 4 * NPAIR + 1):
                        high(1 - g, u - 1, 1)
                    if on(nu, 0, 4 * NPAIR):
                        act.wait_ge(s_sh, u + 1)
                        after(act, s_pT, u * 2 - 2)
                        act.activation(pr[:, g, :, :].rearrange("p (k h) c -> p k (h c)", k=2), S[:, 2 * g:2 * g + 2, :],
                                       ACT.Exp).then_inc(s_pr, 1)
                    if on(nu, 1, 4 * NPAIR + 1):
                        act.wait_ge(s_sub, u)
                        act.activation(prl[:, 1 - g, 4:8, :].rearrange("p h q -> p (h q)"), PT[:, 1, :],
                                       ACT.Identity, scale=PSCALE).then_inc(s_pl1, 1)
                    nb = None if n is None else 2 * n + s // 2 - 2
                    if g == 0 and on(nb, 0, NB):
                        act.wait_ge(s_oT, h * 2 + (s // 2 - 1))
                        act.activation(oT, M0[:, 0:P], ACT.Identity).then_inc(s_oTc, 1)

            for n in range(4):
                pair(n, n)
            with act.Fori(4, NPAIR - 1) as h:
                pair(h, None)
            for n in range(NPAIR - 1, NPAIR + 3):
                pair(n, n)

            act.wait_ge(s_wd, 16)
            for par in range(2):
                act.wait_ge(s_kx[par], 64 * NPAIR)
            for e in range(E):
                act.activation(wdh[:, e], wd[:, e], ACT.Identity, scale=WSCALE).then_inc(s_wdh, 1)
            act.wait_ge(s_padr, 1)
            padding(act, range(E // 2, E))

            def tile_high(j, par):
                act.wait_ge(s_tT, j + 1)
                after(act, s_u, j * 2 - 2)
                act.activation(xth[:, par], (M0 if par == 0 else M1)[:, 0:TW], ACT.Identity).then_inc(s_th, 1)

            def silu(j, hf):
                act.wait_ge(s_g, j * 2 + (hf + 1))
                after(act, s_h, j * 2 + (hf - 1))
                act.activation(sg[:, hf, :], S[:, hf, :], ACT.Silu, scale=1.0 / WSCALE).then_inc(s_sg, 1)

            def hidden_high(j, hf, par):
                act.wait_ge(s_h, j * 2 + (hf + 1))
                after(act, s_y, j - 1)
                act.activation(hidh[:, 2 * par + hf], hid[:, 2 * par + hf], ACT.Identity).then_inc(s_hh, 1)

            def weigh(j, ring, par, left):
                act.wait_ge(s_y, j + 1)
                after(act, s_add[(ring - 2) % XR], left)
                for h in range(2):
                    ins = act.activation(yw[:, par, h, :], PT[:, par, h * P:h * P + P], ACT.Copy,
                                         scale=xt[:, ring, h, P + 1:P + 2])
                ins.then_inc(s_yw, 1)

            def tile(j, r, left, first=False, last=False):
                silu(j, 0)
                if not last:
                    tile_high(j + 1, 1 - r % 2)
                hidden_high(j, 0, r % 2)
                silu(j, 1)
                hidden_high(j, 1, r % 2)
                if not first:
                    weigh(j - 1, (r - 1) % XR, 1 - r % 2, left)

            tile_high(0, 0)
            for j in range(XR):
                tile(j, j, 32 if j >= 3 else 0, first=j == 0)
            with act.Fori(1, NT // XR) as h:
                for r in range(XR):
                    tile(h * XR + r, r, h * 32 + (32 if r >= 3 else 0))
            for j in range(NT // XR * XR, NT):
                tile(j, j % XR, 32 * ((j - 3) // XR + 1), last=j == NT - 1)
            weigh(NT - 1, (NT - 1) % XR, (NT - 1) % 2, 32 * ((NT - 3) // XR + 1))

        @block.vector
        def _(dve):
            steps = [0]

            def link(ins):
                steps[0] += 1
                ins.then_inc(s_st, 1)
                dve.wait_ge(s_st, steps[0])

            def moments(hf):
                for c in range(2):
                    dve.wait_ge(s_x[2 * hf + c], 16)
                    for b in range(16 * hf + 8 * c, 16 * hf + 8 * c + 8):
                        ins = dve.bn_stats(stats[:, b, :], x[:, b, :])
                link(ins)
                for b in range(16 * hf, 16 * hf + 16):
                    ins = dve.bn_aggr(mv[:, b, :], stats[:, b, :])
                ins.then_inc(s_var, 1)
                dve.wait_ge(s_var, hf + 1)

            def inverse_root(hf):
                n, r = nr[:, 16 * hf:16 * hf + 16], rstd[:, 16 * hf:16 * hf + 16]
                link(dve.tensor_scalar(n, mv[:, 16 * hf:16 * hf + 16, 1], EPS, None, ALU.add))
                dve.wait_ge(s_rt, hf + 1)
                link(dve.reciprocal(r, sd[:, 16 * hf:16 * hf + 16]))
                link(dve.tensor_tensor(n, n, r, ALU.mult))
                link(dve.tensor_tensor(n, n, r, ALU.mult))
                link(dve.tensor_scalar(n, n, -0.5, 1.5, ALU.mult, ALU.add))
                link(dve.tensor_tensor(r, r, n, ALU.mult))

            dve.wait_ge(s_setq, 2)
            moments(0)
            dve.wait_ge(s_w, 112)
            dve.tensor_scalar(bob[:], ones[:], bias[:, 2:3], None, ALU.mult).then_inc(s_set, 1)
            dve.tensor_scalar(bqs[:], bias[:, 0:1], SCORE_SCALE, None, ALU.mult)
            link(dve.tensor_scalar(wq[:], wq[:], SCORE_SCALE, None, ALU.mult))
            inverse_root(0)
            dve.tensor_copy(identb[:], identf[:])
            dve.tensor_scalar(nident[:], identf[:], -1.0 / PSCALE, None, ALU.mult)
            dve.tensor_copy(onesb[:], ones[:])
            dve.wait_ge(s_c, 80)
            dve.tensor_copy(upperb[:], upperf[:])
            for h in range(3):
                dve.tensor_copy(mask4[:, h, :], maskf[:])
            link(dve.tensor_copy(mask4[:, 3, :], maskf[:]))
            dve.wait_ge(s_setp, 1)
            dve.tensor_copy(bob[:], M0[:, 0:P])
            dve.tensor_scalar(maskf[:], identf[:], bias[:, 3:4], None, ALU.mult).then_inc(s_set, 1)
            dve.wait_ge(s_setp, 2)
            dve.wait_ge(s_set, 2)
            dve.tensor_tensor(bob[:], M0[:, 0:P], bob[:], ALU.add).then_inc(s_set, 1)

            def normalise(i):
                after(dve, s_xnT, i)
                for j in range(GB):
                    ins = dve.tensor_scalar(xn[:, j, :], x[:, bass.ds(i * GB + j, 1), :].rearrange("p a d -> p (a d)"),
                                            mv[:, bass.ds(i * GB + j, 1), 0], rstd[:, bass.ds(i * GB + j, 1)],
                                            ALU.subtract, ALU.mult)
                ins.then_inc(s_xn, 1)

            def keys_values(i):
                dve.wait_ge(s_hi, i * 2 + 1)
                dve.scalar_tensor_tensor(lo[:, 0, :], M0[:], bias[:, 1:2], hi[:, 0, :], ALU.add, ALU.subtract).then_inc(s_lo, 1)
                dve.wait_ge(s_v, i + 1)
                dve.scalar_tensor_tensor(v1[:, bass.ds(i * GB, GB), :, DK + 1:2 * DK + 1],
                                         M1[:].rearrange("p (b h d) -> p b h d", b=GB, h=H), VSCALE,
                                         v1[:, bass.ds(i * GB, GB), :, 0:DK], ALU.mult, ALU.subtract).then_inc(s_vl, 1)

            def queries(i):
                dve.wait_ge(s_hi, i * 2 + 2)
                dve.scalar_tensor_tensor(lo[:, 1, :], PT[:, 1, :], bqs[:, 0:1], hi[:, 1, :], ALU.add, ALU.subtract).then_inc(s_lo, 1)

            def stacked(i, w):
                for g in (1, 3):
                    dve.wait_ge(s_stk, i * 8 + (4 * w + g + 1))
                    dve.tensor_copy((qc if w else kc)[:, g, bass.ds(i * GT, GT)], S[:, g, :]).then_inc(s_stkv, 1)

            def project(i, last=False):
                stacked(i, 0)
                keys_values(i + 1)
                if not last:
                    normalise(i + 2)
                stacked(i, 1)
                queries(i + 1)

            normalise(0)
            moments(1)
            keys_values(0)
            normalise(1)
            queries(0)
            inverse_root(1)
            for h in range(HU):
                dve.tensor_scalar(sel8[:, h, :], ones[:], identf[:, h:h + 1], None, ALU.mult)
            project(0)
            with dve.Fori(1, NG - 2) as i:
                project(i)
            project(NG - 2, last=True)
            stacked(NG - 1, 0)
            stacked(NG - 1, 1)

            def maxima(g, u):
                dve.wait_ge(s_sc, u + 1)
                dve.tensor_reduce(negm[:, g, :], S[:, 2 * g:2 * g + 2, :].rearrange("p k (h c) -> p (k h) c", h=4),
                                  AX_X, ALU.max, negate=True).then_inc(s_nm, 1)

            def gather(g, u):
                dve.wait_ge(s_pv, u + 1)
                po = M1[:, 0:HU * VW].rearrange("p (h d) -> p h d", h=HU)
                dve.reciprocal(rsum[:, g, :], po[:, :, DK])
                dve.tensor_reduce(osum[:, g], M1[:, 0:HU * VW].rearrange("p (h a d) -> p h d a", h=HU, a=2)[:, :, 0:DK, :],
                                  AX_X, ALU.add).then_inc(s_rs, 1)

            def norm(g, b2, u):
                dve.wait_ge(s_rs, u + 1)
                dve.tensor_tensor(o[:, b2, g * 64:g * 64 + 64].rearrange("p (h d) -> p h d", h=HU), osum[:, g],
                                  rsum[:, g, :].unsqueeze(2).to_broadcast([P, HU, DK]), ALU.mult).then_inc(s_no, 1)


            def statistics(h, step):
                q = h - 2
                if step == 0:
                    after(dve, s_rows, q)
                    dve.wait_ge(s_x2, h * 2 - 2)
                    for j in range(2):
                        ins = dve.bn_stats(st2[:, j, :], x[:, bass.ds(q * 2 + j, 1), :].rearrange("p a d -> p (a d)"))
                    ins.then_inc(s_ra, 1)
                elif step == 1:
                    settle(dve, s_ra, q * 4 + 1, s_spare_dve)
                    for j in range(2):
                        ins = dve.bn_aggr(mv2[:, j, :], st2[:, j, :])
                    ins.then_inc(s_ra, 1)
                elif step == 2:
                    dve.wait_ge(s_ra, q * 4 + 2)
                    dve.tensor_scalar(var2[:], mv2[:, :, 1], EPS, None, ALU.add).then_inc(s_ra, 1)
                elif step == 3:
                    dve.wait_ge(s_ra, q * 4 + 3)
                    dve.tensor_scalar(seed[:].bitcast(I32), var2[:].bitcast(I32), 1, None,
                                      ALU.arith_shift_right).then_inc(s_ra, 1)
                elif step == 4:
                    dve.wait_ge(s_ra, q * 4 + 4)
                    dve.tensor_scalar(seed[:].bitcast(I32), seed[:].bitcast(I32), -1.0, float(MAGIC),
                                      ALU.mult, ALU.add).then_inc(s_seed, 1)

            def choose(h, step):
                q = h - 3
                if step == 0:
                    dve.tensor_copy(lg[:].rearrange("p b e -> p (b e)"), M1[:, LOGI:LOGI + 2 * E]).then_inc(s_lgc, 1)
                elif step == 1:
                    settle(dve, s_lgc, q + 1, s_spare_dve)
                    for j in range(2):
                        ins = dve.max(top[:, j, :], lg[:, j, :])
                    ins.then_inc(s_mx, 1)
                elif step == 2:
                    settle(dve, s_mx, q * 2 + 1, s_spare_dve)
                    for j in range(2):
                        ins = dve.max_index(topi[:, j, :], top[:, j, :], lg[:, j, :])
                    ins.then_inc(s_mx, 1)
                    dve.tensor_tensor(dif[:], top[:, :, 1], top[:, :, 0], ALU.subtract)
                elif step == 3:
                    dve.wait_ge(s_mx, q * 2 + 2)
                    dve.tensor_tensor(hot[:], topi[:, :, 0:2].rearrange("p b k -> p k b").unsqueeze(3).to_broadcast([P, 2, 2, E]),
                                      c_iota.unsqueeze(1).unsqueeze(1).to_broadcast([P, 2, 2, E]), ALU.is_equal).then_inc(s_top, 1)

            def weights(h, ring, step):
                q = h - 3
                w1 = rows[:, ring, :, 0, P + 1]
                w2 = rows[:, ring, :, 1, P + 1]
                if step == 2:
                    dve.wait_ge(s_ed, q + 1)
                    dve.tensor_scalar(den[:], edif[:], WSCALE * HSCALE, WSCALE * HSCALE, ALU.mult, ALU.add).then_inc(s_rw, 1)
                elif step == 3:
                    dve.wait_ge(s_rw, q * 2 + 1)
                    dve.reciprocal(w1, den[:]).then_inc(s_rw, 1)
                elif step == 4:
                    dve.wait_ge(s_rw, q * 2 + 2)
                    dve.tensor_tensor(w2, edif[:], w1, ALU.mult)

            def positions(h, ring, step):
                q = h - 3
                if step == 0:
                    dve.tensor_tensor(posf[:], M1[:, RANK:RANK + 2 * E].rearrange("p (b e) -> p b e", b=2),
                                      c_reg.unsqueeze(1).to_broadcast([P, 2, E]), ALU.add).then_inc(s_rkc, 1)
                elif step == 2:
                    dve.wait_ge(s_rkc, q + 1)
                    for k in range(2):
                        ins = dve.tensor_tensor(prod[:, k, :], hot[:, k].rearrange("p b e -> p (b e)"),
                                                posf[:].rearrange("p b e -> p (b e)"), ALU.mult)
                    ins.then_inc(s_pp, 1)
                elif step == 3:
                    dve.wait_ge(s_pp, q * 2 + 1)
                    dve.tensor_reduce(posk[:], prod[:].rearrange("p k (b e) -> p k b e", b=2), AX_X, ALU.add).then_inc(s_pp, 1)
                elif step == 4:
                    dve.wait_ge(s_pp, q * 2 + 2)
                    dve.tensor_copy(posi[:, ring], posk[:]).then_inc(s_pos, 1)

            def pair(h, n, par):
                def route(s, step):
                    if s == 0 and on(n, 2, NPAIR + 2):
                        statistics(h, step)
                    if s == 1 and on(n, 3, NPAIR + 3):
                        choose(h, step)
                    if s == 2 and on(n, 3, NPAIR + 3):
                        weights(h, 1 - par, step)
                    if s == 3 and on(n, 3, NPAIR + 3):
                        positions(h, 1 - par, step)

                for s in range(4):
                    g, u = s % 2, h * 4 + s
                    nu = None if n is None else 4 * n + s
                    b = h * 2 + (s // 2 - 2)
                    nb = None if n is None else 2 * n + s // 2 - 2
                    if g == 1 and on(n, 3, NPAIR + 3):
                        dve.wait_ge(s_lg if s == 1 else s_rk, h - 2)
                    if on(nu, 0, 4 * NPAIR):
                        dve.wait_ge(s_mT, u + 1)
                        after(dve, s_sh, u)
                        dve.tensor_copy(negmT[0:HU, :], M1[0:HU, 256:256 + P]).then_inc(s_mTc, 1)
                    route(s, 0)
                    if on(nu, 3, 4 * NPAIR + 3):
                        gather(1 - g, u - 3)
                    route(s, 1)
                    if on(nu, 3, 4 * NPAIR + 3):
                        after(dve, s_oT, h * 2 + ((s - 3) // 2 - 1))
                        norm(1 - g, (s - 3) // 2 % 2, u - 3)
                    route(s, 2)
                    if on(nu, 1, 4 * NPAIR + 1):
                        after(dve, s_pv, u - 2)
                        dve.wait_ge(s_pTa, u * 2 - 1)
                        dve.scalar_tensor_tensor(prl[:, 1 - g, 0:4, :].rearrange("p h q -> p (h q)"), PT[:, 0, :], PSCALE,
                                                 prh[:, 1 - g, 0:4, :].rearrange("p h q -> p (h q)"),
                                                 ALU.mult, ALU.subtract).then_inc(s_pTv, 1)
                    route(s, 3)
                    if on(nu, 0, 4 * NPAIR - 1):
                        maxima(1 - g, u + 1)
                    if g == 1 and on(nb, 0, NB):
                        xb = x[:, bass.ds(b, 1), :].rearrange("p a d -> p (a d)")
                        dve.wait_ge(s_pj, b + 1)
                        dve.tensor_tensor(xb, M0[:, P:2 * P], xb, ALU.add).then_inc(s_x2, 1)
                    route(s, 4)

            maxima(0, 0)
            for n in range(4):
                pair(n, n, n % 2)
            with dve.Fori(2, (NPAIR - 2) // 2) as hh:
                pair(hh * 2, None, 0)
                pair(hh * 2 + 1, None, 1)
            for n in range(NPAIR - 2, NPAIR + 3):
                pair(n, n, n % 2)

            chain = [0]

            def link(ins):
                chain[0] += 1
                ins.then_inc(s_tot, 1)
                dve.wait_ge(s_tot, chain[0])

            dve.wait_ge(s_tt, 1)
            link(dve.tensor_copy(tot, M1[:, 0:E]))
            link(dve.tensor_scalar(toti, tot, float(TW - 1), None, ALU.add))
            link(dve.tensor_scalar(toti, toti, TW.bit_length() - 1, None, ALU.arith_shift_right))
            link(dve.tensor_copy(tiles, toti))
            link(dve.tensor_tensor(tri, c_tri.rearrange("p (e f) -> p e f", e=E), tiles.unsqueeze(1).to_broadcast([P, E, E]), ALU.mult))
            link(dve.tensor_reduce(ends, tri, AX_X, ALU.add))
            link(dve.tensor_scalar(step, tiles, -float(TW), float(REG), ALU.mult, ALU.add))
            link(dve.tensor_scalar(gw[:, :, 0], c_row, 1.0 / TW, None, ALU.mult))
            link(dve.tensor_tensor(ge, gw[:, :, 0:1].to_broadcast([P, NT, E]), ends.unsqueeze(1).to_broadcast([P, NT, E]), ALU.is_ge))
            link(dve.tensor_tensor(gw, ge, step.unsqueeze(1).to_broadcast([P, NT, E]), ALU.mult))
            link(dve.tensor_reduce(eidf, ge, AX_X, ALU.add))
            link(dve.tensor_reduce(srcf, gw, AX_X, ALU.add))
            link(dve.tensor_scalar(eidi, eidf, float(E - 1), None, ALU.min))
            link(dve.tensor_tensor(srcf, srcf, c_row, ALU.add))
            link(dve.tensor_scalar(srci, srcf, float(DUMP), None, ALU.min))
            dve.tensor_tensor(padi, tot, c_reg, ALU.add).then_inc(s_tab, 1)

            for e in range(E):
                dve.wait_ge(s_wdh, e + 1)
                dve.scalar_tensor_tensor(wdl[:, e], wd[:, e], WSCALE, wdh[:, e], ALU.mult, ALU.subtract).then_inc(s_wdl, 1)

            def tile_low(j, par):
                dve.wait_ge(s_th, j + 1)
                dve.tensor_tensor(xtl[:, par], (M0 if par == 0 else M1)[:, 0:TW], xth[:, par], ALU.subtract).then_inc(s_tl, 1)

            def hidden(j, hf, par):
                dve.wait_ge(s_sg, j * 2 + (hf + 1))
                dve.wait_ge(s_u, j * 2 + (hf + 1))
                dve.scalar_tensor_tensor(hid[:, 2 * par + hf, :, :].rearrange("p c t -> p (c t)"), S[:, 2 + hf, :],
                                         HSCALE / WSCALE, sg[:, hf, :], ALU.mult, ALU.mult).then_inc(s_h, 1)

            def hidden_low(j, hf, par):
                dve.wait_ge(s_hh, j * 2 + (hf + 1))
                dve.tensor_tensor(hidl[:, 2 * par + hf], hid[:, 2 * par + hf], hidh[:, 2 * par + hf],
                                  ALU.subtract).then_inc(s_hl, 1)

            def tile(j, r, last=False):
                hidden(j, 0, r % 2)
                if not last:
                    tile_low(j + 1, 1 - r % 2)
                hidden_low(j, 0, r % 2)
                hidden(j, 1, r % 2)
                hidden_low(j, 1, r % 2)

            tile_low(0, 0)
            for j in range(4):
                tile(j, j)
            with dve.Fori(1, NT // 4) as h:
                for r in range(4):
                    tile(h * 4 + r, r)
            for j in range(NT // 4 * 4, NT):
                tile(j, j % 4, last=j == NT - 1)

            def finish(i, ring, count):
                dve.wait_ge(s_yin[ring], count)
                xb = x[:, i * GB:i * GB + GB, :]
                dve.tensor_tensor(xb, xb, yin[:, ring, 0], ALU.add).then_inc(s_fs, 1)
                dve.wait_ge(s_fs, i + 1)
                dve.tensor_tensor(xb, xb, yin[:, ring, 1], ALU.add).then_inc(s_fin, 1)

            for i in range(NG):
                finish(i, i % 4, 32 + 32 * (i // 4))

_NAMES = ["x", "ctxT", "wqT", "wkT", "wvT", "woT", "bias", "gateT", "wgT", "wuT", "wdT",
          "ident", "mask", "upper", "small", "stackq", "stackk"]


def kernel(x, ctx_1024, L0_xattn_w_q, L0_xattn_b_q, L0_xattn_w_k, L0_xattn_b_k, L0_xattn_w_v, L0_xattn_b_v,
           L0_xattn_w_o, L0_xattn_b_o, L0_ffn_gate_w, L0_ffn_wg, L0_ffn_wu, L0_ffn_wd):
    import numpy as np
    import concourse.bacc as bacc
    from concourse.bass_utils import run_bass_kernel_spmd

    c = np.ascontiguousarray
    stack = np.zeros((2, P, 2, HG, P), np.float16)
    for h in range(H):
        g, s = h // 4, h % 4
        for d in range(DK):
            for t in range(4):
                stack[0, h * DK + d, t // 2, g, 32 * s + DK * t + d] = 1.0
                stack[1, h * DK + d, t % 2, g, 32 * s + DK * t + d] = 1.0
    r = np.arange(P)
    small = np.concatenate([
        np.broadcast_to(np.arange(E), (P, E)),
        np.broadcast_to(np.arange(E) * REG, (P, E)),
        np.broadcast_to(np.tril(np.ones((E, E))).reshape(-1), (P, E * E)),
        np.broadcast_to(np.arange(NT) * TW, (P, NT)),
        np.stack([r, r + P], 1)], 1).astype(np.float32)
    arrays = {
        "x": c(x),
        "ctxT": c(np.asarray(ctx_1024).reshape(T, P).T),
        "wqT": c(np.asarray(L0_xattn_w_q).T), "wkT": c(np.asarray(L0_xattn_w_k).T),
        "wvT": c(np.asarray(L0_xattn_w_v).T), "woT": c(np.asarray(L0_xattn_w_o).T),
        "bias": c(np.stack([np.asarray(v) for v in (L0_xattn_b_q, L0_xattn_b_k, L0_xattn_b_v, L0_xattn_b_o)], 1)),
        "gateT": c(np.asarray(L0_ffn_gate_w).T),
        "wgT": c(np.asarray(L0_ffn_wg).transpose(2, 0, 1).reshape(P, E * FF)),
        "wuT": c(np.asarray(L0_ffn_wu).transpose(2, 0, 1).reshape(P, E * FF)),
        "wdT": c(np.asarray(L0_ffn_wd).transpose(2, 0, 1).reshape(FC, P, E, P).transpose(1, 2, 0, 3).reshape(P, E * FC * P)),
        "ident": np.eye(P, dtype=np.float32),
        "mask": np.where(r[None, :] <= r[:, None], 0.0, -1e30).astype(np.float32),
        "upper": (r[:, None] < r[None, :]).astype(np.float32),
        "small": c(small),
        "stackq": c(stack[0].reshape(P, -1)), "stackk": c(stack[1].reshape(P, -1)),
    }
    nc = bacc.Bacc("TRN2", target_bir_lowering=False, num_devices=1)
    aps = {n: nc.dram_tensor(f"in_{n}", arrays[n].shape, mybir.dt.from_np(arrays[n].dtype), kind="ExternalInput").ap()
           for n in _NAMES}
    out = nc.dram_tensor("out_0", (NB, P, P), F32, kind="ExternalOutput").ap()
    build(nc, aps, out)
    res = run_bass_kernel_spmd(nc, [{f"in_{n}": arrays[n] for n in _NAMES}], core_ids=[0])
    return res.results[0]["out_0"]
```
